# Optimizing a Trainium2 kernel written in Bass

```python
import numpy as np
import jax
import jax.numpy as jnp

def _softmax(x, axis=-1):
    return jax.nn.softmax(x, axis=axis)

def _gelu(x):
    return jax.nn.gelu(x, approximate=True)

def _silu(x):
    return jax.nn.silu(x)

def _sigmoid(x):
    return jax.nn.sigmoid(x)

def _layernorm(x, axis=-1, eps=1e-05):
    m = jnp.mean(x, axis=axis, keepdims=True)
    v = jnp.var(x, axis=axis, keepdims=True)
    return (x - m) / jnp.sqrt(v + eps)

def _scatter_add(tgt, idx, src, axis=0):
    return tgt.at[idx].add(src)

def _segment_sum(src, seg, n):
    return jax.ops.segment_sum(src, seg, n)
kernel_name = 'mk_gnn_preln_d2_gnn_r32_3cc7de'

def setup_inputs(seed: int=0):
    np.random.seed(seed)
    _w = jnp.asarray

    def _rec_inputs():
        import jax
        import jax.numpy as jnp
        _gk = jax.random.key(seed)
        x = -0.0003713 + 1 * jax.random.normal(jax.random.fold_in(_gk, 1), (50000, 128), jnp.float32)
        src = jax.random.randint(jax.random.fold_in(_gk, 2), (50000,), 0, 50000, jnp.int32)
        dst = jax.random.randint(jax.random.fold_in(_gk, 3), (50000,), 0, 50000, jnp.int32)
        _o = jnp.argsort(dst, stable=True)
        src = src[_o]
        dst = dst[_o]
        edge_attr_128 = -4.21973e-05 + 0.999841 * jax.random.normal(jax.random.fold_in(_gk, 12), (50000, 128), jnp.float32)
        return (x, src, dst, edge_attr_128)
    x, src, dst, edge_attr_128 = _rec_inputs()

    def _L0_gnn_setup():
        import jax, jax.numpy as jnp
        import numpy as np
        N_NODES = 3125
        N_EDGES = 18750
        D = 128
        key = jax.random.key(seed)
        ks = jax.random.split(key, 8)
        nodes = jax.random.normal(ks[0], (N_NODES, D), dtype=jnp.float32)
        edges = jax.random.normal(ks[1], (N_EDGES, D), dtype=jnp.float32)
        senders = jax.random.randint(ks[2], (N_EDGES,), 0, N_NODES, dtype=jnp.int32)
        receivers = jax.random.randint(ks[3], (N_EDGES,), 0, N_NODES, dtype=jnp.int32)
        W_node = jax.random.normal(ks[4], (D, D), dtype=jnp.float32) / np.sqrt(D)
        b_node = jnp.zeros((D,), dtype=jnp.float32)
        W_edge = jax.random.normal(ks[5], (D, D), dtype=jnp.float32) / np.sqrt(D)
        b_edge = jnp.zeros((D,), dtype=jnp.float32)
        root_emb = jax.random.normal(ks[6], (1, D), dtype=jnp.float32)
        return {'nodes': nodes, 'edges': edges, 'senders': senders, 'receivers': receivers, 'W_node': W_node, 'b_node': b_node, 'W_edge': W_edge, 'b_edge': b_edge, 'root_emb': root_emb}
    _L0_gnn_all = _L0_gnn_setup()
    _L0_gnn_in = {k: v for k, v in _L0_gnn_all.items() if k in ('W_node', 'b_node', 'W_edge', 'b_edge', 'root_emb')}
    del _L0_gnn_all

    def _L1_gnn_setup():
        import jax, jax.numpy as jnp
        import numpy as np
        N = 3125
        E = 50000
        IN_DIM = 128
        HID = 128
        key = jax.random.key(seed)
        k1, k2, k3, k4, k5 = jax.random.split(key, 5)
        h = jax.random.normal(k1, (N, IN_DIM), dtype=jnp.float32)
        weight = jax.random.normal(k2, (2 * IN_DIM, HID), dtype=jnp.float32) * (1.0 / np.sqrt(2 * IN_DIM))
        bias = jax.random.normal(k3, (HID,), dtype=jnp.float32) * 0.01
        src = jax.random.randint(k4, (E,), 0, N, dtype=jnp.int32)
        dst = jax.random.randint(k5, (E,), 0, N, dtype=jnp.int32)
        return {'h': h, 'weight': weight, 'bias': bias, 'src': src, 'dst': dst}
    _L1_gnn_all = _L1_gnn_setup()
    _L1_gnn_in = {k: v for k, v in _L1_gnn_all.items() if k in ('weight', 'bias')}
    del _L1_gnn_all
    return {'x': x, 'src': src, 'dst': dst, 'edge_attr_128': edge_attr_128, 'L0_gnn_W_node': _L0_gnn_in['W_node'], 'L0_gnn_b_node': _L0_gnn_in['b_node'], 'L0_gnn_W_edge': _L0_gnn_in['W_edge'], 'L0_gnn_b_edge': _L0_gnn_in['b_edge'], 'L0_gnn_root_emb': _L0_gnn_in['root_emb'], 'L1_gnn_weight': _L1_gnn_in['weight'], 'L1_gnn_bias': _L1_gnn_in['bias']}

def reference(x, src, dst, edge_attr_128, L0_gnn_W_node, L0_gnn_b_node, L0_gnn_W_edge, L0_gnn_b_edge, L0_gnn_root_emb, L1_gnn_weight, L1_gnn_bias):
    import jax
    import jax.numpy as jnp

    def _L0_gnn_ref(nodes, edges, senders, receivers, W_node, b_node, W_edge, b_edge, root_emb):
        import jax, jax.numpy as jnp
        import numpy as np
        N_NODES = 3125
        N_EDGES = 18750
        D = 128
        n = nodes.shape[0]
        transf = nodes @ W_node + b_node
        edg = edges @ W_edge + b_edge
        ones = jnp.ones(senders.shape[0], dtype=jnp.float32)
        sender_degree = jax.ops.segment_sum(ones, senders, num_segments=n) + 1.0
        receiver_degree = jax.ops.segment_sum(ones, receivers, num_segments=n) + 1.0
        norm = (jax.lax.rsqrt(sender_degree)[senders] * jax.lax.rsqrt(receiver_degree)[receivers])[:, None]
        msgs = norm * jax.nn.relu(transf[senders] + edg)
        agg = jax.ops.segment_sum(msgs, receivers, num_segments=n)
        agg = agg + jax.nn.relu(transf + root_emb) / receiver_degree[:, None]
        return jax.nn.relu(agg)

    def _L1_gnn_ref(h, weight, bias, src, dst):
        import jax, jax.numpy as jnp
        import numpy as np
        N = 3125
        E = 50000
        IN_DIM = 128
        HID = 128
        n = h.shape[0]
        deg = jax.ops.segment_sum(jnp.ones_like(dst, dtype=h.dtype), dst, num_segments=n)
        norm = jnp.power(jnp.clip(deg, 1.0, None), -0.5)[:, None]
        fh = h * norm
        agg = jax.ops.segment_sum(fh[src], dst, num_segments=n) * norm
        cat = jnp.concatenate([h, agg], axis=1)
        out = cat @ weight + bias
        nrm = jnp.sqrt(jnp.sum(out * out, axis=1, keepdims=True))
        return out / nrm
    h = jnp.maximum(_layernorm(x, axis=-1), 0.0)
    x = x + _L0_gnn_ref(h, edge_attr_128, src, dst, L0_gnn_W_node, L0_gnn_b_node, L0_gnn_W_edge, L0_gnn_b_edge, L0_gnn_root_emb)
    h = jnp.maximum(_layernorm(x, axis=-1), 0.0)
    x = x + _L1_gnn_ref(h, L1_gnn_weight, L1_gnn_bias, src, dst)
    return x

_drawn_inputs = setup_inputs


def setup_inputs(seed=0):
    import zlib

    import numpy as np

    out = dict(_drawn_inputs(seed))
    spreads = {'L0_gnn_b_node': (0.0, 0.1), 'L0_gnn_b_edge': (0.0, 0.321)}
    factors = {'L1_gnn_bias': 53.249}
    for name, (base, spread) in spreads.items():
        noise = np.random.default_rng([zlib.crc32(name.encode()), seed]).standard_normal(out[name].shape)
        drawn = base * np.exp(spread * noise) if base else spread * noise
        out[name] = jnp.asarray(drawn.astype(out[name].dtype))
    for name, factor in factors.items():
        out[name] = (out[name] * factor).astype(out[name].dtype)
    return out
```

```python
import concourse.bass as bass
from concourse import mybir
from contextlib import ExitStack

P = 128
D = 128
NODES = 50000
EDGES = 50000
T = 4
GROUPS = -(-NODES // (P * T))
TILES = GROUPS * T
ROWS = TILES * P
RING = 32
SPAN = 3
LAG = 4
BACK, AHEAD = 8, 13
U = 4
PEEL = 3
EPS = 1e-5
W0 = D + 1


def gnn_kernel(nc: bass.Bass, x, edgeT, srcT, dstT, dst_cur, dst_next, dst_first, group_tile_in, w_node,
               b_node, w_edge, b_edge, root, w_out, b_out, ident_in, iota_in, tile_base_in, before_in, out):
    f32, bf16, f16, i32 = mybir.dt.float32, mybir.dt.bfloat16, mybir.dt.float16, mybir.dt.int32
    ALU = mybir.AluOpType
    ACT = mybir.ActivationFunctionType
    AX = mybir.AxisListType.X

    table0 = nc.dram_tensor("table0", [2 * ROWS + P, W0], f32).ap()
    table1 = nc.dram_tensor("table1", [2 * ROWS + P, D], f32).ap()
    x1_dram = nc.dram_tensor("x1_dram", [ROWS, D], f32).ap()

    def rows4(t, g):
        return t[bass.ds(g * (T * P), T * P), :].rearrange("(j p) f -> p j f", p=P)

    ctx = ExitStack()
    with ctx:
        def sb(name, shape, dt=f32):
            return ctx.enter_context(nc.sbuf_tensor(name, shape, dt))

        def sem(name):
            return ctx.enter_context(nc.semaphore(name))

        a_row = sb("a_row", [1, TILES + 4], i32)
        flag_i = sb("flag_i", [1, 4], i32)
        ident = sb("ident", [P, P])
        iota = sb("iota", [P, TILES + 4])
        tile_base = sb("tile_base", [P, TILES + 4])
        neg_base = sb("neg_base", [P, TILES + 4])
        iota_h = sb("iota_h", [P, TILES], f16)
        src_i = sb("src_i", [P, TILES], i32)
        dst_i = sb("dst_i", [P, TILES], i32)
        src_use = sb("src_use", [P, TILES], i32)
        dst_f = sb("dst_f", [P, TILES])
        dst_use = sb("dst_use", [P, TILES + 4])
        part_i = sb("part_i", [P, TILES], i32)
        digits = sb("digits", [P, 4, TILES])
        c_send = sb("c_send", [P, TILES])
        rn = sb("rn", [P, TILES])
        rinv = sb("rinv", [P, TILES])
        norm1 = sb("norm1", [P, TILES])
        rstd1 = sb("rstd1", [P, TILES])
        nb1 = sb("nb1", [P, TILES])
        deg = sb("deg", [P, 3, TILES])
        dsq = sb("dsq", [P, 3, TILES])
        cur_i = sb("cur_i", [P, TILES], i32)
        next_i = sb("next_i", [P, TILES], i32)
        cur_f = sb("cur_f", [P, TILES])
        next_f = sb("next_f", [P, TILES])
        before = sb("before", [P, P + 1])
        z_edge = sb("z_edge", [P, P])
        z_rows = sb("z_rows", [P, W0])
        z_pre = sb("z_pre", [P, D])
        z_msg = sb("z_msg", [P, W0])
        z_node = sb("z_node", [P, P])
        z_same = sb("z_same", [P, P])
        z_dup = sb("z_dup", [P, P])
        z_cnt = sb("z_cnt", [P, 4])
        z_src = sb("z_src", [P, 1], i32)
        z_dst = sb("z_dst", [P, 1], i32)
        z_sum = sb("z_sum", [P, W0])
        z_scr = sb("z_scr", [P, 4], i32)
        first_i = sb("first_i", [TILES // 4, 4], i32)
        first_f = sb("first_f", [TILES // 4, 4])
        cmp = sb("cmp", [P, 4, TILES + 1])
        a_f = sb("a_f", [P, TILES + 1])
        bad = sb("bad", [P, 8])
        group_tile = sb("group_tile", [P, TILES])
        badrow = sb("badrow", [P, 2, TILES])
        ones = sb("ones", [P, P])
        ones3 = sb("ones3", [3, P], bf16)
        eps_t = sb("eps_t", [P, 1])
        wn = sb("wn", [P, D])
        we = sb("we", [P, D])
        w1 = sb("w1", [P, 2, D])
        brow = sb("brow", [3, 4, D])
        bsum = sb("bsum", [3, 3, D])
        bres = sb("bres", [3, 3, D])
        idx = sb("idx", [P, 4, T], i32)
        bpart = sb("bpart", [3, 3, 3, D], bf16)
        bsel = sb("bsel", [3, 3, D])
        bias4 = sb("bias4", [3, 3, T, D], bf16)
        oneh = sb("oneh", [P, 2, T, 2, P + TILES], bf16)

        xb = sb("xb", [P, 8, T, D])
        ya = sb("ya", [P, 4, T, W0])
        h = sb("h", [P, 4, T, D])
        agg = sb("agg", [P, 2, T, D])
        hT = sb("hT", [P, 2, T * P])
        aT = sb("aT", [P, 2, T * P])
        gath = sb("gath", [P, 4, T, W0])
        edge = sb("edge", [P, 4, T * P])
        pre = sb("pre", [P, 2, T, D])
        ring = sb("ring", [P, RING, D])
        pick = sb("pick", [P, 2, T, SPAN, P])
        q = sb("q", [P, 2, T, D])
        v = sb("v", [P, T, D])
        x1 = sb("x1", [P, 4, T, D])
        bnst = sb("bnst", [P, 2, T, 6])
        mv = sb("mv", [P, 4, T, 2])
        sd = sb("sd", [P, 4, T])
        rs = sb("rs", [P, 4, T])
        nb = sb("nb", [P, 4, T])
        sc1 = sb("sc1", [P, 4, T])
        bi1 = sb("bi1", [P, 4, T])
        junk = sb("junk", [P, T, D])
        ss = sb("ss", [P, 4, T])
        nrm = sb("nrm", [P, 4, T])
        inv = sb("inv", [P, 4, T])

        bank = [ctx.enter_context(nc.psum_tensor(f"bank{i}", [P, 512], f32)) for i in range(8)]

        names = """consts_in idx_in cmp_rdy setup ones_rdy a_psum bad_psum flag_rdy tables_rdy deg_sum deg_sqrt
            hot_rdy hist_done x_in0 x_in1 x_in2 x_in3 n_bn n_stats n_sd n_rs n_coef n_h n_tp n_hT n_mm
            n_evac n_col t0_out0 t0_out1 t0_out2 t0_out3 idx_rdy
            g_in0 g_in1 g_in2 g_in3 e_in0 e_in1 e_in2 e_in3 y_in0 y_in1 y_in2 y_in3 xl_in0 xl_in1 xl_in2
            xl_in3 emm_done pre_rdy msg_rdy pick_rdy seg_done q_rdy v_rdy x1_rdy l_bn l_stats l_sd l_rs
            l_nb l_coef t1_rdy l0_out0 l0_out1 l0_out2 l0_out3
            r_in0 r_in1 r_in2 r_in3 xx_in0 xx_in1 xx_in2 xx_in3 o_pick o_seg o_agg o_h o_tp o_hT o_aT
            o_mm o_sq o_nrm o_inv o_y y_out0 y_out1 y_out2 y_out3
            z0_zero z0_init z0_edge z0_idx z0_src z0_emm z0_tgt z0_msg z0_same z0_sum z0_scat z0_mvin z0_mvout z0_carry z0_reset
            z1_zero z1_init z1_edge z1_idx z1_src z1_emm z1_tgt z1_msg z1_same z1_sum z1_scat z1_mvin z1_mvout z1_carry z_first""".split()
        S = {n: sem(n) for n in names}

        def need(eng, s, value):
            if isinstance(value, int) and value <= 0:
                return
            eng.wait_ge(s, value)

        def rounds(eng, step, lag, unroll=U, peel=PEEL):
            full = GROUPS // unroll
            for i in range(peel):
                for u in range(unroll):
                    step(i, u)
            with eng.Fori(peel, full) as i:
                for u in range(unroll):
                    step(i, u)
            for s in range(full * unroll, GROUPS + lag):
                step(s // unroll, s % unroll)

        def grp(i, u, lag, unroll=U):
            g = i * unroll + (u - lag)
            if isinstance(g, int) and not 0 <= g < GROUPS:
                return None
            return g, (u - lag) % unroll, i + (u - lag) // unroll

        LAPS = [len(range(k, GROUPS, 4)) for k in range(4)]

        def x_of(i, u, lag, j=None):
            s = i * U + (u - lag)
            if isinstance(s, int):
                ap = xb[:, s % 8, :, :]
                return ap if j is None else xb[:, s % 8, j, :]
            if j is None:
                return xb[:, bass.ds(s & 7, 1), :, :].rearrange("p o j f -> p (o j) f")
            return xb[:, bass.ds(s & 7, 1), j, :].rearrange("p o f -> p (o f)")

        def ring_of(i, u, lag, j):
            s = i * U + (u - lag)
            if isinstance(s, int):
                return ring[:, (s * T + j) % RING, :]
            return ring[:, bass.ds((s * T + j) & (RING - 1), 1), :].rearrange("p o f -> p (o f)")

        def eng_values(eng, row):
            return nc.values_load_multi_w_load_instructions(row, engines=(eng.engine,), min_val=0,
                                                            max_val=TILES - 1)[1]

        block = ctx.enter_context(nc.Block())

        def flag_of(eng):
            eng.wait_ge(S["flag_rdy"], 1)
            return eng.value_load(flag_i[0:1, 0:1], min_val=0, max_val=1 << 10)

        def general_loads(sp, layer):
            table = (table0, table1)[layer]
            w = (W0, D)[layer]
            z = {n: S[f"z{layer}_{n}"] for n in ("zero", "init", "edge", "scat", "mvin", "mvout")}
            zeros, low, high = gath[:, 0, :, 0:w], gath[:, 1, :, 0:w], gath[:, 2, :, 0:w]
            sp.wait_ge(z["zero"], 1)
            sp.dma_start(table[2 * ROWS:, :], gath[:, 0, 0, 0:w]).then_inc(z["init"], 16)
            with sp.Fori(GROUPS, 2 * GROUPS) as g:
                sp.dma_start(rows4(table, g), zeros).then_inc(z["init"], 16)
            if layer == 0:
                sp.dma_start(z_edge[:, :], edgeT[:, 0:P]).then_inc(z["edge"], 16)
                with sp.Fori(1, TILES) as k:
                    sp.wait_ge(z["scat"], k * 16)
                    sp.dma_start(z_edge[:, :], edgeT[:, bass.ds(k * P, P)]).then_inc(z["edge"], 16)
            sp.wait_ge(z["scat"], 16 * TILES)

            def move(g):
                sp.dma_start(low, rows4(table, g)).then_inc(z["mvin"], 16)
                sp.dma_start(high, rows4(table, g + GROUPS)).then_inc(z["mvin"], 16)
                sp.wait_ge(z["mvin"], g * 32 + 32)
                sp.dma_start(rows4(table, g), high).then_inc(z["mvout"], 16)
                sp.dma_start(rows4(table, g + GROUPS), low).then_inc(z["mvout"], 16)

            move(0)
            with sp.Fori(1, GROUPS) as g:
                sp.wait_ge(z["mvout"], g * 32)
                move(g)
            sp.wait_ge(z["mvout"], 32 * GROUPS)

        def own_rows(sp, bad_n, n):
            first = n * (T * P) + (bad_n > 0) * ROWS
            return table0[bass.ds(first, T * P), :].rearrange("(j p) f -> p j f", p=P)

        def general_gathers(pool, layer):
            table = (table0, table1)[layer]
            w = (W0, D)[layer]
            z = {n: S[f"z{layer}_{n}"] for n in ("init", "idx", "src", "sum", "scat", "mvout", "carry")}
            pool.wait_ge(z["init"], 16 * (GROUPS + 1))

            def tile(k):
                pool.wait_ge(z["idx"], k + 1)
                nc.gpsimd.tensor_tensor(z_scr[:, 0:1], z_scr[:, 2:3], z_scr[:, 3:4], ALU.add).then_inc(
                    z["carry"], 1)
                pool.indirect_dma_start(
                    out=z_rows[:, 0:w], out_offset=None, in_=table[0:ROWS, :],
                    in_offset=bass.IndirectOffsetOnAxis(ap=z_src[:, :], axis=0),
                    bounds_check=ROWS - 1, oob_is_err=False).then_inc(z["src"], 16)
                pool.wait_ge(z["sum"], k + 1)
                nc.gpsimd.tensor_tensor(z_scr[:, 1:2], z_scr[:, 2:3], z_scr[:, 3:4], ALU.add).then_inc(
                    z["carry"], 1)
                pool.indirect_dma_start(
                    in_=z_sum[:, 0:w], in_offset=None, out=table[:, :],
                    out_offset=bass.IndirectOffsetOnAxis(ap=z_dst[:, :], axis=0),
                    bounds_check=2 * ROWS + P - 1, oob_is_err=True,
                    compute_op=ALU.add).then_inc(z["scat"], 16)

            with pool.Fori(0, TILES) as k:
                tile(k)
            pool.wait_ge(z["mvout"], 32 * GROUPS)
            if layer == 0:
                pool.wait_ge(S["z0_reset"], 1)

        def general_vector(dve, layer):
            V = nc.vector
            w = (W0, D)[layer]
            z = {n: S[f"z{layer}_{n}"] for n in ("zero", "idx", "src", "emm", "tgt", "same", "sum", "scat", "carry")}
            V.memset(gath[:, 0, :, 0:D], 0.0)
            V.memset(gath[:, 0, :, D:], 1.0)
            V.memset(z_scr[:, :], 0)
            V.memset(z_msg[:, D:], 0.0).then_inc(z["zero"], 1)

            def tile(k, first=False):
                if not first:
                    dve.wait_ge(z["scat"], k * 16)
                    dve.wait_ge(z["carry"], k * 2)
                V.tensor_copy(z_src[:, :], src_i[:, bass.ds(k, 1)])
                V.tensor_copy(z_node[:, :], dst_f[:, bass.ds(k, 1)].to_broadcast([P, P])).then_inc(z["idx"], 1)
                dve.wait_ge(z["emm"], k + 1)
                V.tensor_scalar(z_same[:, :], bank[5][:, 0:P], dst_f[:, bass.ds(k, 1)], None,
                                ALU.is_equal).then_inc(z["tgt"], 1)
                dve.wait_ge(z["src"], k * 16 + 16)
                if layer == 0:
                    V.tensor_tensor(z_pre[:, :], bank[7][:, 0:D], z_rows[:, 0:D], ALU.add)
                else:
                    V.tensor_copy(z_msg[:, 0:D], z_rows[:, 0:D])
                dve.wait_ge(z["tgt"], k * 5 + 1)
                V.tensor_tensor(z_dup[:, :], z_same[:, :], before[:, 0:P], ALU.mult).then_inc(z["tgt"], 1)
                dve.wait_ge(z["tgt"], k * 5 + 2)
                V.reduce_sum(z_cnt[:, 0:1], z_dup[:, :], AX)
                V.tensor_scalar(z_cnt[:, 1:2], dst_f[:, bass.ds(k, 1)], before[:, P:], -float(ROWS),
                                ALU.subtract, ALU.add).then_inc(z["tgt"], 1)
                dve.wait_ge(z["tgt"], k * 5 + 3)
                V.scalar_tensor_tensor(z_cnt[:, 2:3], z_cnt[:, 0:1], 0.0, z_cnt[:, 1:2],
                                       ALU.is_equal, ALU.mult).then_inc(z["tgt"], 1)
                dve.wait_ge(z["tgt"], k * 5 + 4)
                V.tensor_scalar(z_dst[:, :], z_cnt[:, 2:3], before[:, P:], 2.0 * ROWS, ALU.add,
                                ALU.add).then_inc(z["tgt"], 1)
                dve.wait_ge(z["same"], k + 1)
                dve.wait_ge(z["tgt"], k * 5 + 5)
                V.tensor_copy(z_sum[:, 0:w], bank[6][:, 0:w]).then_inc(z["sum"], 1)

            tile(0, True)
            with dve.Fori(1, TILES) as k:
                tile(k)
            dve.wait_ge(z["scat"], 16 * TILES)
            if layer == 0:
                V.tensor_scalar(dst_use[:, 0:TILES], tile_base[:, 0:TILES], before[:, P:], None, ALU.add)
                V.memset(we[:, :], 0.0)
                V.memset(bias4[:, 1, :, :], 0.0)
                V.tensor_scalar(a_row[0:1, 0:TILES], iota[0:1, 0:TILES], -1.0, 0.0, ALU.add,
                                ALU.max).then_inc(S["z_first"], 1)
                dve.wait_ge(S["z_first"], 1)
                V.tensor_copy(src_use[:, :], dst_use[:, 0:TILES]).then_inc(S["z0_reset"], 1)
                dve.wait_ge(S["z0_reset"], 1)

        def general_products(pe, layer):
            w = (W0, D)[layer]
            z = {n: S[f"z{layer}_{n}"] for n in ("idx", "edge", "emm", "tgt", "msg", "same")}

            def tile(k):
                pe.wait_ge(z["idx"], k + 1)
                if layer == 0:
                    pe.wait_ge(z["edge"], k * 16 + 16)
                    nc.tensor.matmul(bank[7][:, 0:D], ones3[:, :], bias4[:, 1, 0, :], start=True, stop=False)
                    nc.tensor.matmul(bank[7][:, 0:D], z_edge[:, :], we[:, :], start=False, stop=True)
                nc.tensor.transpose(bank[5][:, 0:P], z_node[:, :], ident[:, :]).then_inc(z["emm"], 1)
                if layer == 0:
                    pe.wait_ge(z["msg"], k + 1)
                pe.wait_ge(z["tgt"], k * 5 + 2)
                nc.tensor.matmul(bank[6][:, 0:w], z_same[:, :], z_msg[:, 0:w], start=True,
                                 stop=True).then_inc(z["same"], 1)

            with pe.Fori(0, TILES) as k:
                tile(k)
            if layer == 0:
                pe.wait_ge(S["z0_reset"], 1)

        def general_messages(act):
            z = {n: S[f"z0_{n}"] for n in ("tgt", "msg")}
            with act.Fori(0, TILES) as k:
                act.wait_ge(z["tgt"], k * 5 + 2)
                nc.scalar.activation(z_msg[:, 0:D], z_pre[:, :], ACT.Relu,
                                     scale=z_rows[:, D:]).then_inc(z["msg"], 1)

        @block.sync
        def _(sp):
            for dst, src in ((before, before_in), (ident, ident_in), (iota, iota_in), (tile_base, tile_base_in), (wn, w_node),
                             (we, w_edge), (group_tile, group_tile_in)):
                sp.dma_start(dst[:, :], src).then_inc(S["consts_in"], 16)
            sp.dma_start(w1[:, :, :], w_out.rearrange("(k p) f -> p k f", p=P)).then_inc(S["consts_in"], 16)
            for r in range(3):
                for k, b in enumerate((b_node, b_edge, root, b_out)):
                    sp.dma_start(brow[r:r + 1, k, :], b).then_inc(S["consts_in"], 16)
            for dst, src in ((src_i, srcT), (dst_i, dstT), (cur_i, dst_cur), (next_i, dst_next),
                             (first_i, dst_first)):
                sp.dma_start(dst[:, :], src).then_inc(S["idx_in"], 16)

            def load_nodes(i, u):
                g = grp(i, u, 0)
                if g:
                    g, slot, r = g
                    need(sp, S["n_h"], g - 3)
                    sp.dma_start(xb[:, slot, :, :], rows4(x, g)).then_inc(S[f"x_in{slot}"], 16)

            rounds(sp, load_nodes, 0)

            for k in range(4):
                sp.wait_ge(S[f"t0_out{k}"], 16 * LAPS[k])

            bad_n = flag_of(sp)
            with sp.If(bad_n > 0):
                general_loads(sp, 0)

            def load_layer0(i, u):
                g = grp(i, u, 0)
                if g:
                    g, slot, r = g
                    need(sp, S["emm_done"], g - 3)
                    sp.dma_start(edge[:, slot, :], edgeT[:, bass.ds(g * (T * P), T * P)]).then_inc(
                        S[f"e_in{slot}"], 16)
                n = grp(i, u, 2)
                if n:
                    n, slot, r = n
                    need(sp, S["q_rdy"], n - 3)
                    sp.dma_start(ya[:, slot, :, :], own_rows(sp, bad_n, n)).then_inc(S[f"y_in{slot}"], 16)
                    need(sp, S["x1_rdy"], n - 3)
                    sp.dma_start(xb[:, slot, :, :], rows4(x, n)).then_inc(S[f"xl_in{slot}"], 16)

            sp.wait_ge(S["n_h"], GROUPS)
            rounds(sp, load_layer0, 2)

            for k in range(4):
                sp.wait_ge(S[f"l0_out{k}"], 32 * LAPS[k])

            with sp.If(bad_n > 0):
                general_loads(sp, 1)

            def load_layer1(i, u):
                g = grp(i, u, 0, 8)
                if g:
                    g, slot, r = g
                    need(sp, S["o_y"], g - 7)
                    need(sp, S[f"xx_in{slot % 4}"], 16 * (2 * r + slot // 4))
                    sp.dma_start(xb[:, slot, :, :], rows4(x1_dram, g)).then_inc(S[f"xx_in{slot % 4}"], 16)

            sp.wait_ge(S["x1_rdy"], GROUPS)
            rounds(sp, load_layer1, 0, 8, 1)

        @block.gpsimd
        def _(pool):
            def gather(dst, table, col, landed):
                pool.indirect_dma_start(
                    out=dst, out_offset=None, in_=table,
                    in_offset=bass.IndirectOffsetOnAxis(ap=col, axis=0),
                    bounds_check=ROWS - 1, oob_is_err=False).then_inc(landed, 16)

            for k in range(4):
                pool.wait_ge(S[f"t0_out{k}"], 16 * LAPS[k])

            bad_n = flag_of(pool)
            with pool.If(bad_n > 0):
                general_gathers(pool, 0)

            def place_indices(g, slot):
                nc.gpsimd.tensor_copy(idx[:, slot, :], src_use[:, bass.ds(g * T, T)]).then_inc(
                    S["idx_rdy"], 1)

            def fetch0(i, u):
                g = grp(i, u, 0)
                if g:
                    g, slot, r = g
                    pool.wait_ge(S["idx_rdy"], g + 1)
                    need(pool, S["msg_rdy"], g - 3)
                    n = grp(i, u, -1)
                    if n:
                        need(pool, S[f"g_in{n[1]}"], 64 * n[2])
                        place_indices(*n[:2])
                    for j in range(T):
                        gather(gath[:, slot, j, :], table0[0:ROWS, :], idx[:, slot, j:j + 1], S[f"g_in{slot}"])

            place_indices(0, 0)
            rounds(pool, fetch0, 0)

            for k in range(4):
                pool.wait_ge(S[f"l0_out{k}"], 32 * LAPS[k])
                pool.wait_ge(S[f"g_in{k}"], 64 * LAPS[k])
            pool.wait_ge(S["seg_done"], GROUPS)

            with pool.If(bad_n > 0):
                general_gathers(pool, 1)

            def fetch1(i, u):
                g = grp(i, u, 0, 8)
                if g:
                    g, slot, r = g
                    pool.wait_ge(S["idx_rdy"], GROUPS + g + 1)
                    need(pool, S["o_seg"], g - (LAG + 1))
                    n = grp(i, u, -1, 8)
                    if n:
                        need(pool, S[f"r_in{n[1] % 4}"], 64 * (2 * n[2] + n[1] // 4))
                        place_indices(n[0], n[1] % 4)
                    for j in range(T):
                        gather(ring[:, slot * T + j, :], table1[0:ROWS, :], idx[:, slot % 4, j:j + 1],
                               S[f"r_in{slot % 4}"])

            place_indices(0, 0)
            rounds(pool, fetch1, 0, 8, 1)

        @block.vector
        def _(dve):
            chain = [0]

            def link(ins):
                chain[0] += 1
                ins.then_inc(S["setup"], 1)
                dve.wait_ge(S["setup"], chain[0])

            V = nc.vector
            link(V.memset(ones3[:, :], 1.0))
            link(V.memset(eps_t[:, :], EPS))
            link(V.memset(dst_use[:, TILES:], -1.0))
            V.memset(ones[:, :], 1.0).then_inc(S["ones_rdy"], 1)
            dve.wait_ge(S["consts_in"], 16 * 20)
            dve.wait_ge(S["idx_in"], 16 * 5)
            link(V.tensor_copy(iota_h[:, :], iota[:, 0:TILES]))
            link(V.tensor_scalar(neg_base[:, :], tile_base[:, :], -1.0, None, ALU.mult))
            for k, ids in enumerate((src_i, dst_i)):
                link(V.tensor_single_scalar(part_i[:, :], ids[:, :], P - 1, ALU.bitwise_and))
                link(V.tensor_copy(digits[:, 2 * k, :], part_i[:, :]))
                link(V.tensor_single_scalar(part_i[:, :], ids[:, :], 7, ALU.logical_shift_right))
                link(V.tensor_copy(digits[:, 2 * k + 1, :], part_i[:, :]))
            link(V.tensor_copy(dst_use[:, 0:TILES], dst_i[:, :]))
            link(V.tensor_copy(dst_f[:, :], dst_i[:, :]))
            link(V.tensor_copy(src_use[:, :], src_i[:, :]))
            link(V.tensor_copy(first_f[:, :], first_i[:, :]))
            for c in range(4):
                ins = V.tensor_scalar(cmp[0:TILES // 4, c, :], tile_base[0:TILES // 4, 0:TILES + 1],
                                      first_f[:, c:c + 1], None, ALU.is_gt)
            ins.then_inc(S["cmp_rdy"], 1)
            link(V.tensor_copy(cur_f[:, :], cur_i[:, :]))
            link(V.tensor_copy(next_f[:, :], next_i[:, :]))
            link(V.tensor_tensor(badrow[:, 0, :], cur_f[:, :], next_f[:, :], ALU.is_gt))
            link(V.reduce_max(bad[:, 0:1], badrow[:, 0, :], AX))
            dve.wait_ge(S["a_psum"], 1)
            link(V.tensor_scalar(a_f[:, :], bank[0][:, 0:TILES + 1], -1.0, 0.0, ALU.add, ALU.max))
            link(V.tensor_copy(a_row[0:1, 0:TILES], a_f[0:1, 0:TILES]))
            link(V.tensor_tensor(badrow[:, 0, :], a_f[:, 1:TILES + 1], a_f[:, 0:TILES], ALU.subtract))
            link(V.tensor_scalar(badrow[:, 0, :], badrow[:, 0, :], SPAN - 1.0, None, ALU.is_gt))
            link(V.reduce_max(bad[:, 1:2], badrow[:, 0, :], AX))
            link(V.tensor_tensor(badrow[:, 0, :], a_f[:, 0:TILES], group_tile[:, :], ALU.subtract))
            link(V.tensor_scalar(badrow[:, 1, :], badrow[:, 0, :], -float(BACK), None, ALU.is_lt))
            link(V.reduce_max(bad[:, 2:3], badrow[:, 1, :], AX))
            link(V.tensor_scalar(badrow[:, 1, :], badrow[:, 0, :], float(AHEAD), None, ALU.is_gt))
            link(V.reduce_max(bad[:, 3:4], badrow[:, 1, :], AX))
            V.reduce_sum(bad[:, 4:5], bad[:, 0:4], AX).then_inc(S["bad_psum"], 1)

            link(V.tensor_tensor(bsum[:, 0, :], brow[:, 0, :], brow[:, 2, :], ALU.add))
            link(V.tensor_tensor(bsum[:, 1, :], brow[:, 1, :], brow[:, 2, :], ALU.subtract))
            link(V.tensor_copy(bsum[:, 2, :], brow[:, 3, :]))
            link(V.tensor_copy(bpart[:, 0, :, :], bsum[:, :, :]))
            link(V.tensor_tensor(bres[:, :, :], bsum[:, :, :], bpart[:, 0, :, :], ALU.subtract))
            link(V.tensor_copy(bpart[:, 1, :, :], bres[:, :, :]))
            link(V.tensor_tensor(bres[:, :, :], bres[:, :, :], bpart[:, 1, :, :], ALU.subtract))
            link(V.tensor_copy(bpart[:, 2, :, :], bres[:, :, :]))
            link(V.tensor_scalar(bsel[:, :, :], bpart[:, 0, :, :], ident[0:3, 0:1], None, ALU.mult))
            link(V.scalar_tensor_tensor(bsel[:, :, :], bpart[:, 1, :, :], ident[0:3, 1:2], bsel[:, :, :],
                                        ALU.mult, ALU.add))
            link(V.scalar_tensor_tensor(bsel[:, :, :], bpart[:, 2, :, :], ident[0:3, 2:3], bsel[:, :, :],
                                        ALU.mult, ALU.add))
            for j in range(T):
                ins = V.tensor_copy(bias4[:, :, j, :], bsel[:, :, :])
            link(ins)
            dve.wait_ge(S["bad_psum"], 2)
            V.tensor_copy(flag_i[0:1, 0:1], bank[1][0:1, 0:1]).then_inc(S["flag_rdy"], 1)

            def one_hots(i, u):
                g = grp(i, u, 0)
                if g:
                    g, slot, r = g
                    need(dve, S["hist_done"], g - 1)
                    for j in range(T):
                        for k in range(2):
                            V.tensor_scalar(oneh[:, slot % 2, j, k, 0:P], iota_h[:, 0:P],
                                            digits[:, 2 * k, bass.ds(g * T + j, 1)], None, ALU.is_equal)
                            ins = V.tensor_scalar(oneh[:, slot % 2, j, k, P:], iota_h[:, :],
                                                  digits[:, 2 * k + 1, bass.ds(g * T + j, 1)], None,
                                                  ALU.is_equal)
                    ins.then_inc(S["hot_rdy"], 1)

            rounds(dve, one_hots, 0)
            dve.wait_ge(S["hist_done"], GROUPS)
            V.tensor_scalar(deg[:, 0, :], bank[2][:, 0:TILES], 1.0, None, ALU.add)
            V.tensor_scalar(deg[:, 1, :], bank[3][:, 0:TILES], 1.0, None, ALU.add)
            V.tensor_scalar(deg[:, 2, :], bank[3][:, 0:TILES], 1.0, None, ALU.max).then_inc(S["deg_sum"], 1)
            dve.wait_ge(S["deg_sum"], 1)
            V.reciprocal(rinv[:, :], deg[:, 1, :])
            dve.wait_ge(S["deg_sqrt"], 1)
            V.reciprocal(c_send[:, :], dsq[:, 0, :])
            V.reciprocal(rn[:, :], dsq[:, 1, :])
            V.reciprocal(norm1[:, :], dsq[:, 2, :]).then_inc(S["tables_rdy"], 1)
            dve.wait_ge(S["tables_rdy"], 1)

            def node_step(i, u):
                g = grp(i, u, 1)
                if g:
                    g, slot, r = g
                    dve.wait_ge(S["n_sd"], g + 1)
                    V.reciprocal(rs[:, slot, :], sd[:, slot, :]).then_inc(S["n_rs"], 1)
                    dve.wait_ge(S["n_rs"], g + 1)
                    V.scalar_tensor_tensor(nb[:, slot, :], mv[:, slot, :, 0], -1.0, rs[:, slot, :],
                                           ALU.mult, ALU.mult).then_inc(S["n_coef"], 1)
                g = grp(i, u, 0)
                if g:
                    g, slot, r = g
                    dve.wait_ge(S[f"x_in{slot}"], 16 * (r + 1))
                    for j in range(T):
                        ins = V.bn_stats(bnst[:, slot % 2, j, :], xb[:, slot, j, :])
                    ins.then_inc(S["n_bn"], 1)
                g = grp(i, u, 0)
                if g:
                    g, slot, r = g
                    dve.wait_ge(S["n_bn"], g + 1)
                    need(dve, S["n_h"], g - 3)
                g = grp(i, u, 3)
                if g:
                    g, slot, r = g
                    dve.wait_ge(S["n_tp"], g + 1)
                    need(dve, S["n_mm"], g - 1)
                    V.tensor_copy(hT[:, slot % 2, :], bank[4 + slot % 2][:, :]).then_inc(S["n_hT"], 1)
                g = grp(i, u, 5)
                if g:
                    g, slot, r = g
                    need(dve, S[f"t0_out{slot}"], 16 * r)
                    V.tensor_copy(ya[:, slot, :, D], c_send[:, bass.ds(g * T, T)]).then_inc(S["n_col"], 1)
                g = grp(i, u, 0)
                if g:
                    g, slot, r = g
                    for j in range(T):
                        ins = V.bn_aggr(mv[:, slot, j, :], bnst[:, slot % 2, j, :])
                    ins.then_inc(S["n_stats"], 1)

            rounds(dve, node_step, 5)

            def coefficients(n, slot):
                at = bass.ds(n * T, T)
                dve.wait_ge(S["l_sd"], n + 1)
                V.reciprocal(rstd1[:, at], sd[:, slot, :]).then_inc(S["l_rs"], 1)
                dve.wait_ge(S["l_rs"], n + 1)
                V.scalar_tensor_tensor(nb1[:, at], mv[:, slot, :, 0], -1.0, rstd1[:, at],
                                       ALU.mult, ALU.mult).then_inc(S["l_nb"], 1)
                V.tensor_tensor(sc1[:, slot, :], rstd1[:, at], norm1[:, at], ALU.mult)
                dve.wait_ge(S["l_nb"], n + 1)
                V.tensor_tensor(bi1[:, slot, :], nb1[:, at], norm1[:, at], ALU.mult).then_inc(S["l_coef"], 1)

            def picks(n, par, first, ready):
                for j in range(T):
                    for w in range(SPAN):
                        ins = V.tensor_scalar(pick[:, par, j, w, :], iota[:, 0:P],
                                              dst_use[:, bass.ds(first[j] + w, 1)],
                                              neg_base[:, bass.ds(n * T + j, 1)], ALU.subtract, ALU.is_equal)
                ins.then_inc(ready, 1)

            def firsts(eng, n):
                at = a_row[0:1, n * T:n * T + T] if isinstance(n, int) else a_row[0:1, bass.ds(n * T, T)]
                return eng_values(eng, at)

            for k in range(4):
                dve.wait_ge(S[f"t0_out{k}"], 16 * LAPS[k])
            bad_n = flag_of(dve)
            with dve.If(bad_n > 0):
                general_vector(dve, 0)

            def layer0_step(i, u):
                n = grp(i, u, 6)
                if n:
                    coefficients(*n[:2])
                g = grp(i, u, 0)
                if g:
                    g, slot, r = g
                    dve.wait_ge(S[f"g_in{slot}"], 64 * (r + 1))
                    dve.wait_ge(S["emm_done"], g + 1)
                    need(dve, S["msg_rdy"], g - 1)
                    V.tensor_tensor(pre[:, slot % 2, :, :],
                                    bank[slot % 2][:, :].rearrange("p (j f) -> p j f", f=D),
                                    gath[:, slot, :, 0:D], ALU.add).then_inc(S["pre_rdy"], 1)
                n = grp(i, u, 5)
                if n:
                    n, slot, r = n
                    dve.wait_ge(S["seg_done"], n + 1)
                    dve.wait_ge(S["q_rdy"], n + 1)
                    for j in range(T):
                        ins = V.scalar_tensor_tensor(v[:, j, :], bank[2 + slot % 2][:, j * D:(j + 1) * D],
                                                     rn[:, bass.ds(n * T + j, 1)], q[:, slot % 2, j, :],
                                                     ALU.mult, ALU.add)
                    ins.then_inc(S["v_rdy"], 1)
                    dve.wait_ge(S["v_rdy"], n + 1)
                    dve.wait_ge(S[f"xl_in{slot}"], 16 * (r + 1))
                    need(dve, S[f"l0_out{slot}"], 32 * r)
                    V.scalar_tensor_tensor(x1[:, slot, :, :], v[:, :, :], 0.0, xb[:, slot, :, :],
                                           ALU.max, ALU.add).then_inc(S["x1_rdy"], 1)
                    dve.wait_ge(S["x1_rdy"], n + 1)
                    for j in range(T):
                        ins = V.bn_stats(bnst[:, slot % 2, j, :], x1[:, slot, j, :])
                    ins.then_inc(S["l_bn"], 1)
                    dve.wait_ge(S["l_bn"], n + 1)
                n = grp(i, u, 3)
                if n:
                    n, slot, r = n
                    need(dve, S["seg_done"], n - 1)
                    picks(n, slot % 2, firsts(dve, n), S["pick_rdy"])
                n = grp(i, u, 5)
                if n:
                    n, slot, r = n
                    for j in range(T):
                        ins = V.bn_aggr(mv[:, slot, j, :], bnst[:, slot % 2, j, :])
                    ins.then_inc(S["l_stats"], 1)

            rounds(dve, layer0_step, 6)

            def layer1_step(i, u):
                n = grp(i, u, 0)
                if n:
                    n, slot, r = n
                    need(dve, S["o_seg"], n - 1)
                    picks(n, slot % 2, firsts(dve, n), S["o_pick"])
                n = grp(i, u, 4)
                if n:
                    n, slot, r = n
                    dve.wait_ge(S["o_tp"], n + 1)
                    need(dve, S["o_mm"], n - 1)
                    V.tensor_copy(hT[:, slot % 2, :], bank[6 + slot % 2][:, :]).then_inc(S["o_hT"], 1)
                n = grp(i, u, 6)
                if n:
                    n, slot, r = n
                    dve.wait_ge(S["o_nrm"], n + 1)
                    V.reciprocal(inv[:, slot, :], nrm[:, slot, :]).then_inc(S["o_inv"], 1)
                    dve.wait_ge(S["o_inv"], n + 1)
                    need(dve, S[f"y_out{slot}"], 16 * r)
                    for j in range(T):
                        ins = V.scalar_tensor_tensor(x1[:, slot, j, :], bank[2 + slot % 2][:, j * D:(j + 1) * D],
                                                     inv[:, slot, j:j + 1], x_of(i, u, 6, j), ALU.mult, ALU.add)
                    ins.then_inc(S["o_y"], 1)

            for k in range(4):
                dve.wait_ge(S[f"l0_out{k}"], 32 * LAPS[k])
            with dve.If(bad_n > 0):
                general_vector(dve, 1)
            rounds(dve, layer1_step, 7)

        @block.tensor
        def _(pe):
            mm = nc.tensor.matmul
            pe.wait_ge(S["consts_in"], 16 * 20)
            pe.wait_ge(S["cmp_rdy"], 1)
            pe.wait_ge(S["ones_rdy"], 1)
            K = TILES // 4
            for c in range(4):
                ins = mm(bank[0][:, 0:TILES + 1], ones[0:K, :], cmp[0:K, c, :], start=c == 0, stop=c == 3)
            ins.then_inc(S["a_psum"], 1)
            pe.wait_ge(S["bad_psum"], 1)
            mm(bank[1][:, 0:1], ones[:, :], bad[:, 4:5], start=True, stop=True).then_inc(S["bad_psum"], 1)

            def histograms(i, u):
                g = grp(i, u, 0)
                if g:
                    g, slot, r = g
                    pe.wait_ge(S["hot_rdy"], g + 1)
                    for j in range(T):
                        for k in range(2):
                            ins = mm(bank[2 + k][:, 0:TILES], oneh[:, slot % 2, j, k, 0:P],
                                     oneh[:, slot % 2, j, k, P:],
                                     start=isinstance(g, int) and g == 0 and j == 0,
                                     stop=isinstance(g, int) and g == GROUPS - 1 and j == T - 1,
                                     skip_group_check=True)
                    ins.then_inc(S["hist_done"], 1)

            rounds(pe, histograms, 0)

            def node_step(i, u):
                g = grp(i, u, 2)
                if g:
                    g, slot, r = g
                    pe.wait_ge(S["n_h"], g + 1)
                    need(pe, S["n_hT"], g - 1)
                    for j in range(T):
                        ins = nc.tensor.transpose(bank[4 + slot % 2][:, j * P:(j + 1) * P], h[:, slot, j, :],
                                                  ident[:, :])
                    ins.then_inc(S["n_tp"], 1)
                g = grp(i, u, 4)
                if g:
                    g, slot, r = g
                    pe.wait_ge(S["n_hT"], g + 1)
                    need(pe, S["n_evac"], g - 1)
                    affine(bank[6 + slot % 2], 0, [(hT[:, slot % 2, :], wn[:, :])], S["n_mm"])

            def affine(out_bank, b, pairs, done):
                mm(out_bank[:, :], ones3[:, :], bias4[:, b, :, :].rearrange("k j f -> k (j f)"),
                   start=True, stop=False, skip_group_check=True)
                for j in range(T):
                    for rows, w in pairs:
                        ins = mm(out_bank[:, j * D:(j + 1) * D], rows[:, j * P:(j + 1) * P], w,
                                 start=False, stop=True, skip_group_check=True)
                ins.then_inc(done, 1)

            pe.wait_ge(S["flag_rdy"], 1)
            rounds(pe, node_step, 4)

            def firsts(n):
                at = a_row[0:1, n * T:n * T + T] if isinstance(n, int) else a_row[0:1, bass.ds(n * T, T)]
                return eng_values(pe, at)

            def sums(n, par, out_bank, done):
                a = firsts(n)
                for j in range(T):
                    for w in range(SPAN):
                        ins = mm(out_bank[:, j * D:(j + 1) * D], pick[:, par, j, w, :],
                                 ring[:, bass.ds((a[j] + w) & (RING - 1), 1), :].rearrange("p o f -> p (o f)"),
                                 start=w == 0, stop=w == SPAN - 1)
                ins.then_inc(done, 1)

            def layer0_step(i, u):
                g = grp(i, u, 0)
                if g:
                    g, slot, r = g
                    pe.wait_ge(S[f"e_in{slot}"], 16 * (r + 1))
                    need(pe, S["pre_rdy"], g - 1)
                    affine(bank[slot % 2], 1, [(edge[:, slot, :], we[:, :])], S["emm_done"])
                n = grp(i, u, LAG)
                if n:
                    n, slot, r = n
                    pe.wait_ge(S["pick_rdy"], n + 1)
                    if isinstance(n, int):
                        pe.wait_ge(S["msg_rdy"], min(n + LAG, GROUPS))
                    else:
                        pe.wait_ge(S["msg_rdy"], n + LAG)
                    need(pe, S["v_rdy"], n - 1)
                    sums(n, slot % 2, bank[2 + slot % 2], S["seg_done"])

            pe.wait_ge(S["tables_rdy"], 1)
            bad_n = flag_of(pe)
            with pe.If(bad_n > 0):
                pe.wait_ge(S["n_evac"], GROUPS)
                general_products(pe, 0)
            rounds(pe, layer0_step, LAG)

            def layer1_step(i, u):
                n = grp(i, u, 5)
                if n:
                    n, slot, r = n
                    pe.wait_ge(S["o_hT"], n + 1)
                    pe.wait_ge(S["o_aT"], n + 1)
                    need(pe, S["o_y"], n - 1)
                    affine(bank[2 + slot % 2], 2, [(hT[:, slot % 2, :], w1[:, 0, :]),
                                                   (aT[:, slot % 2, :], w1[:, 1, :])], S["o_mm"])
                n = grp(i, u, 3)
                if n:
                    n, slot, r = n
                    pe.wait_ge(S["o_h"], n + 1)
                    pe.wait_ge(S["o_agg"], n + 1)
                    need(pe, S["o_hT"], n - 1)
                    need(pe, S["o_aT"], n - 1)
                    for j in range(T):
                        nc.tensor.transpose(bank[6 + slot % 2][:, j * P:(j + 1) * P], h[:, slot, j, :],
                                            ident[:, :])
                        ins = nc.tensor.transpose(bank[slot % 2][:, j * P:(j + 1) * P],
                                                  agg[:, slot % 2, j, :], ident[:, :])
                    ins.then_inc(S["o_tp"], 1)
                n = grp(i, u, 1)
                if n:
                    n, slot, r = n
                    pe.wait_ge(S["o_pick"], n + 1)
                    if isinstance(n, int) and n == 0:
                        for k in range(LAG - 1):
                            pe.wait_ge(S[f"r_in{k}"], 64)
                    if not (isinstance(n, int) and n + LAG - 1 >= GROUPS):
                        pe.wait_ge(S[f"r_in{(slot + LAG - 1) % 4}"], 64 * (r + (slot + LAG - 1) // 4 + 1))
                    need(pe, S["o_agg"], n - 1)
                    sums(n, slot % 2, bank[4 + slot % 2], S["o_seg"])

            pe.wait_ge(S["v_rdy"], GROUPS)
            pe.wait_ge(S["n_evac"], GROUPS)
            with pe.If(bad_n > 0):
                general_products(pe, 1)
            rounds(pe, layer1_step, 6)

        @block.scalar
        def _(act):
            A = nc.scalar.activation
            act.wait_ge(S["deg_sum"], 1)
            A(dsq[:, :, :], deg[:, :, :], ACT.Sqrt).then_inc(S["deg_sqrt"], 1)

            def node_step(i, u):
                g = grp(i, u, 5)
                if g:
                    g, slot, r = g
                    act.wait_ge(S["n_mm"], g + 1)
                    need(act, S[f"t0_out{slot}"], 16 * r)
                    A(ya[:, slot, :, 0:D], bank[6 + slot % 2][:, :].rearrange("p (j f) -> p j f", f=D),
                      ACT.Copy).then_inc(S["n_evac"], 1)
                g = grp(i, u, 1)
                if g:
                    g, slot, r = g
                    act.wait_ge(S["n_coef"], g + 1)
                    need(act, S["n_tp"], g - 3)
                    for j in range(T):
                        ins = A(h[:, slot, j, :], xb[:, slot, j, :], ACT.Relu, bias=nb[:, slot, j:j + 1],
                                scale=rs[:, slot, j:j + 1])
                    ins.then_inc(S["n_h"], 1)
                g = grp(i, u, 0)
                if g:
                    g, slot, r = g
                    act.wait_ge(S["n_stats"], g + 1)
                    A(sd[:, slot, :], mv[:, slot, :, 1], ACT.Sqrt, bias=eps_t[:, :]).then_inc(S["n_sd"], 1)
                g = grp(i, u, 6)
                if g:
                    g, slot, r = g
                    act.wait_ge(S["n_evac"], g + 1)
                    act.wait_ge(S["n_col"], g + 1)
                    act.dma_start(rows4(table0, g), ya[:, slot, :, :]).then_inc(S[f"t0_out{slot}"], 16)

            rounds(act, node_step, 6)

            def layer0_step(i, u):
                g = grp(i, u, 0)
                if g:
                    g, slot, r = g
                    act.wait_ge(S["pre_rdy"], g + 1)
                    need(act, S["seg_done"], g - (LAG + 1))
                    for j in range(T):
                        ins = A(ring_of(i, u, 0, j), pre[:, slot % 2, j, :], ACT.Relu,
                                scale=gath[:, slot, j, D:D + 1])
                    ins.then_inc(S["msg_rdy"], 1)
                n = grp(i, u, LAG)
                if n:
                    n, slot, r = n
                    act.wait_ge(S[f"y_in{slot}"], 16 * (r + 1))
                    need(act, S["v_rdy"], n - 1)
                    for j in range(T):
                        ins = A(q[:, slot % 2, j, :], ya[:, slot, j, 0:D], ACT.Relu,
                                scale=rinv[:, bass.ds(n * T + j, 1)])
                    ins.then_inc(S["q_rdy"], 1)
                n = grp(i, u, 6)
                if n:
                    n, slot, r = n
                    act.wait_ge(S["l_coef"], n + 1)
                    need(act, S[f"l0_out{slot}"], 32 * r)
                    for j in range(T):
                        ins = A(h[:, slot, j, :], x1[:, slot, j, :], ACT.Relu, bias=bi1[:, slot, j:j + 1],
                                scale=sc1[:, slot, j:j + 1])
                    ins.then_inc(S["t1_rdy"], 1)
                n = grp(i, u, 5)
                if n:
                    n, slot, r = n
                    act.wait_ge(S["l_stats"], n + 1)
                    A(sd[:, slot, :], mv[:, slot, :, 1], ACT.Sqrt, bias=eps_t[:, :]).then_inc(S["l_sd"], 1)
                n = grp(i, u, 7)
                if n:
                    n, slot, r = n
                    act.wait_ge(S["x1_rdy"], n + 1)
                    act.dma_start(rows4(x1_dram, n), x1[:, slot, :, :]).then_inc(S[f"l0_out{slot}"], 16)
                    act.wait_ge(S["t1_rdy"], n + 1)
                    act.dma_start(rows4(table1, n), h[:, slot, :, :]).then_inc(S[f"l0_out{slot}"], 16)

            act.wait_ge(S["tables_rdy"], 1)
            act.wait_ge(S["n_tp"], GROUPS)
            bad_n = flag_of(act)
            with act.If(bad_n > 0):
                general_messages(act)
            rounds(act, layer0_step, 7)

            def layer1_step(i, u):
                n = grp(i, u, 6)
                if n:
                    n, slot, r = n
                    act.wait_ge(S["o_mm"], n + 1)
                    need(act, S["o_inv"], n - 3)
                    for j in range(T):
                        ins = A(junk[:, j, :], bank[2 + slot % 2][:, j * D:(j + 1) * D], ACT.Square,
                                accum_out=ss[:, slot, j:j + 1])
                    ins.then_inc(S["o_sq"], 1)
                    act.wait_ge(S["o_sq"], n + 1)
                    A(nrm[:, slot, :], ss[:, slot, :], ACT.Sqrt).then_inc(S["o_nrm"], 1)
                n = grp(i, u, 2)
                if n:
                    n, slot, r = n
                    act.wait_ge(S["o_seg"], n + 1)
                    need(act, S["o_tp"], n - 1)
                    for j in range(T):
                        ins = A(agg[:, slot % 2, j, :], bank[4 + slot % 2][:, j * D:(j + 1) * D], ACT.Copy,
                                scale=norm1[:, bass.ds(n * T + j, 1)])
                    ins.then_inc(S["o_agg"], 1)
                    act.wait_ge(S[f"xx_in{slot}"], 16 * (r + 1))
                    for j in range(T):
                        ins = A(h[:, slot, j, :], x_of(i, u, 2, j), ACT.Relu,
                                bias=nb1[:, bass.ds(n * T + j, 1)], scale=rstd1[:, bass.ds(n * T + j, 1)])
                    ins.then_inc(S["o_h"], 1)
                n = grp(i, u, 4)
                if n:
                    n, slot, r = n
                    act.wait_ge(S["o_tp"], n + 1)
                    need(act, S["o_mm"], n - 1)
                    A(aT[:, slot % 2, :], bank[slot % 2][:, :], ACT.Copy).then_inc(S["o_aT"], 1)
                n = grp(i, u, 7)
                if n:
                    n, slot, r = n
                    act.wait_ge(S["o_y"], n + 1)
                    act.dma_start(rows4(out, n), x1[:, slot, :, :]).then_inc(S[f"y_out{slot}"], 16)

            for k in range(4):
                act.wait_ge(S[f"l0_out{k}"], 32 * LAPS[k])
            rounds(act, layer1_step, 7)
            for k in range(4):
                act.wait_ge(S[f"y_out{k}"], 16 * LAPS[k])


def kernel(x, src, dst, edge_attr_128, L0_gnn_W_node, L0_gnn_b_node, L0_gnn_W_edge, L0_gnn_b_edge,
           L0_gnn_root_emb, L1_gnn_weight, L1_gnn_bias):
    import numpy as np
    import concourse.bacc as bacc
    from concourse.bass_utils import run_bass_kernel_spmd

    pad = np.arange(NODES, ROWS, dtype=np.int32)
    zero_rows = np.zeros((ROWS - NODES, D), np.float32)
    src_all = np.concatenate([np.asarray(src), pad])
    dst_all = np.concatenate([np.asarray(dst), pad])
    dst_tiles = dst_all.reshape(TILES, P)
    edges = np.concatenate([np.asarray(edge_attr_128), zero_rows])
    tiles = np.arange(TILES + 4, dtype=np.float32)

    def across(row):
        return np.ascontiguousarray(np.broadcast_to(row, (P, row.shape[-1])))

    arrays = {
        "x": np.concatenate([np.asarray(x), zero_rows]),
        "edgeT": np.ascontiguousarray(edges.T),
        "srcT": np.ascontiguousarray(src_all.reshape(TILES, P).T),
        "dstT": np.ascontiguousarray(dst_tiles.T),
        "dst_cur": dst_all.reshape(P, TILES),
        "dst_next": np.concatenate([dst_all[1:], dst_all[-1:]]).reshape(P, TILES),
        "dst_first": np.ascontiguousarray(dst_tiles[:, 0]).reshape(TILES // 4, 4),
        "group_tile": across(np.float32(T) * np.arange(GROUPS, dtype=np.float32).repeat(T)),
        "w_node": np.asarray(L0_gnn_W_node), "b_node": np.asarray(L0_gnn_b_node).reshape(1, D),
        "w_edge": np.asarray(L0_gnn_W_edge), "b_edge": np.asarray(L0_gnn_b_edge).reshape(1, D),
        "root": np.asarray(L0_gnn_root_emb), "w_out": np.asarray(L1_gnn_weight),
        "b_out": np.asarray(L1_gnn_bias).reshape(1, D),
        "ident": np.eye(P, dtype=np.float32),
        "iota": across(tiles),
        "tile_base": across(np.float32(P) * tiles),
        "before": np.concatenate([np.tri(P, k=-1, dtype=np.float32),
                                  np.arange(P, dtype=np.float32).reshape(P, 1)], 1),
    }
    nc = bacc.Bacc("TRN2", target_bir_lowering=False, num_devices=1)
    aps = [nc.dram_tensor(f"in_{k}", a.shape, mybir.dt.from_np(a.dtype), kind="ExternalInput").ap()
           for k, a in arrays.items()]
    out = nc.dram_tensor("out", (ROWS, D), mybir.dt.float32, kind="ExternalOutput").ap()
    gnn_kernel(nc, *aps, out)
    r = run_bass_kernel_spmd(nc, [{f"in_{k}": a for k, a in arrays.items()}], core_ids=[0])
    return r.results[0]["out"][:NODES]
```

```python
import concourse.bass as bass
from concourse import mybir
from contextlib import ExitStack

P = 128
D = 128
NODES = 50000
EDGES = 50000
T = 4
GROUPS = -(-NODES // (P * T))
TILES = GROUPS * T
ROWS = TILES * P
RING = 32
SPAN = 3
LAG = 5
BACK, AHEAD = 8, 13
U = 8
PEEL = 2
EPS = 1e-5
W0 = D + 1


def gnn_kernel(nc: bass.Bass, x, edgeT, srcT, dstT, dst_cur, dst_next, dst_first, group_tile_in, tile_no_in, dst_rows, w_node,
               b_node, w_edge, b_edge, root, w_out, b_out, ident_in, iota_in, tile_base_in, before_in, out):
    f32, bf16, f16, i32 = mybir.dt.float32, mybir.dt.bfloat16, mybir.dt.float16, mybir.dt.int32
    ALU = mybir.AluOpType
    ACT = mybir.ActivationFunctionType
    AX = mybir.AxisListType.X

    table0 = nc.dram_tensor("table0", [2 * ROWS + P, W0], f32).ap()
    table1 = nc.dram_tensor("table1", [2 * ROWS + P, D], f32).ap()
    x1_dram = nc.dram_tensor("x1_dram", [ROWS, D], f32).ap()

    def rows4(t, g):
        return t[bass.ds(g * (T * P), T * P), :].rearrange("(j p) f -> p j f", p=P)

    ctx = ExitStack()
    with ctx:
        def sb(name, shape, dt=f32):
            return ctx.enter_context(nc.sbuf_tensor(name, shape, dt))

        def sem(name):
            return ctx.enter_context(nc.semaphore(name))

        ring_at = sb("ring_at", [1, TILES], i32)
        offs_i = sb("offs_i", [1, TILES], i32)
        flag_i = sb("flag_i", [1, 4], i32)
        ident = sb("ident", [P, P])
        iota = sb("iota", [P, TILES + 4])
        tile_base = sb("tile_base", [P, TILES + 4])
        tile_no = sb("tile_no", [TILES // 4, SPAN, 4])
        dst_rows_i = sb("dst_rows_i", [TILES // 4, 4, P], i32)
        rel = sb("rel", [P, TILES, SPAN])
        count4 = sb("count4", [P, TILES, T], f16)
        src_i = sb("src_i", [P, TILES], i32)
        dst_i = sb("dst_i", [P, TILES], i32)
        src_use = sb("src_use", [P, TILES], i32)
        dst_f = sb("dst_f", [P, TILES])
        part_i = sb("part_i", [P, TILES], i32)
        digits = sb("digits", [P, 4, TILES], f16)
        c_send = sb("c_send", [P, TILES])
        rn = sb("rn", [P, TILES])
        rinv = sb("rinv", [P, TILES])
        norm1 = sb("norm1", [P, TILES])
        rstd1 = sb("rstd1", [P, TILES])
        nb1 = sb("nb1", [P, TILES])
        deg = sb("deg", [P, 3, TILES])
        dsq = sb("dsq", [P, 3, TILES])
        cur_i = sb("cur_i", [P, TILES], i32)
        next_i = sb("next_i", [P, TILES], i32)
        cur_f = sb("cur_f", [P, TILES])
        next_f = sb("next_f", [P, TILES])
        before = sb("before", [P, P + 1])
        z_edge = sb("z_edge", [P, P])
        z_rows = sb("z_rows", [P, W0])
        z_pre = sb("z_pre", [P, D])
        z_msg = sb("z_msg", [P, W0])
        z_node = sb("z_node", [P, P])
        z_same = sb("z_same", [P, P])
        z_dup = sb("z_dup", [P, P])
        z_cnt = sb("z_cnt", [P, 4])
        z_src = sb("z_src", [P, 1], i32)
        z_dst = sb("z_dst", [P, 1], i32)
        z_sum = sb("z_sum", [P, W0])
        z_scr = sb("z_scr", [P, 4], i32)
        first_i = sb("first_i", [TILES // 4, 4], i32)
        first_f = sb("first_f", [TILES // 4, 4])
        a_f = sb("a_f", [P, TILES + 1])
        bad = sb("bad", [P, 8])
        group_tile = sb("group_tile", [P, TILES])
        badrow = sb("badrow", [P, 2, TILES])
        ones = sb("ones", [P, P])
        ones3 = sb("ones3", [3, P], bf16)
        eps_t = sb("eps_t", [P, 1])
        wn = sb("wn", [P, D])
        we = sb("we", [P, D])
        w1 = sb("w1", [P, 2, D])
        brow = sb("brow", [3, 4, D])
        bsum = sb("bsum", [3, 3, D])
        bres = sb("bres", [3, 3, D])
        idx = sb("idx", [P, 4, T], i32)
        bpart = sb("bpart", [3, 3, 3, D], bf16)
        bsel = sb("bsel", [3, 3, D])
        bias4 = sb("bias4", [3, 3, T, D], bf16)
        low_hot = sb("low_hot", [P, 2, P, T], bf16)
        high_hot = sb("high_hot", [P, 2, TILES, T], bf16)

        xb = sb("xb", [P, 8, T, D])
        ya = sb("ya", [P, 4, T, W0])
        h = sb("h", [P, 4, T, D])
        agg = sb("agg", [P, 2, T, D])
        hT = sb("hT", [P, 2, T * P])
        aT = sb("aT", [P, 2, T * P])
        gath = sb("gath", [P, 4, T, W0])
        edge = sb("edge", [P, 4, T * P])
        ring = sb("ring", [P, RING + SPAN - 1, D])
        pick = sb("pick", [P, 2, T * SPAN, P])

        ring_flat = ring[:, :, :].rearrange("p r f -> p (r f)")
        cmp = edge[:, :, :].rearrange("p s e -> p (s e)")[:, 0:4 * (TILES + 1)].rearrange(
            "p (c t) -> p c t", c=4)
        chosen = ring_flat[0:TILES // 4, 0:4 * TILES].rearrange("p (c t) -> p c t", c=4)
        offs = ring_flat[0:1, 4 * TILES:5 * TILES]
        dst_rows_f = ring_flat[0:TILES // 4, (RING - 4) * D:RING * D].rearrange("p (c e) -> p c e", c=4)
        q = sb("q", [P, 2, T, D])
        v = sb("v", [P, T, D])
        x1 = sb("x1", [P, 4, T, D])
        bnst = sb("bnst", [P, 2, T, 6])
        mv = sb("mv", [P, 4, T, 2])
        sd = sb("sd", [P, 4, T])
        rs = sb("rs", [P, 4, T])
        nb = sb("nb", [P, 4, T])
        sc1 = sb("sc1", [P, 4, T])
        bi1 = sb("bi1", [P, 4, T])
        junk = sb("junk", [P, T, D])
        ss = sb("ss", [P, 4, T])
        nrm = sb("nrm", [P, 4, T])
        inv = sb("inv", [P, 4, T])

        bank = [ctx.enter_context(nc.psum_tensor(f"bank{i}", [P, 512], f32)) for i in range(8)]

        names = """consts_in idx_in cmp_rdy chosen_rdy rel_psum rel_used setup ones_rdy a_psum bad_psum flag_rdy tables_rdy deg_sum deg_sqrt
            hot_rdy hist_done x_in0 x_in1 x_in2 x_in3 n_bn n_stats n_sd n_rs n_coef n_h n_tp n_hT n_mm
            n_evac n_col t0_out0 t0_out1 t0_out2 t0_out3 idx_rdy
            g_in0 g_in1 g_in2 g_in3 e_in0 e_in1 e_in2 e_in3 y_in0 y_in1 y_in2 y_in3 xl_in0 xl_in1 xl_in2
            xl_in3 emm_done sum_rdy msg_rdy pick_rdy seg_done q_rdy v_rdy x1_rdy l_bn l_stats l_sd l_rs
            l_nb l_coef t1_rdy x1_out0 x1_out1 x1_out2 x1_out3 t1_out0 t1_out1 t1_out2 t1_out3
            r_in0 r_in1 r_in2 r_in3 xx_in0 xx_in1 xx_in2 xx_in3 o_again o_pick o_seg o_agg o_h o_tp o_hT o_aT
            o_mm o_sq o_nrm o_inv o_y y_out0 y_out1 y_out2 y_out3
            z0_zero z0_init z0_edge z0_idx z0_src z0_emm z0_tgt z0_msg z0_same z0_sum z0_scat z0_mvin z0_mvout z0_carry z0_reset
            z1_zero z1_init z1_edge z1_idx z1_src z1_emm z1_tgt z1_msg z1_same z1_sum z1_scat z1_mvin z1_mvout z1_carry z_chain""".split()
        S = {n: sem(n) for n in names}

        def need(eng, s, value):
            if isinstance(value, int) and value <= 0:
                return
            eng.wait_ge(s, value)

        def rounds(eng, step, lag):
            full = GROUPS // U
            for i in range(PEEL):
                for u in range(U):
                    step(i, u)
            with eng.Fori(PEEL, full) as i:
                for u in range(U):
                    step(i, u)
            for s in range(full * U, GROUPS + lag):
                step(s // U, s % U)

        def grp(i, u, lag):
            g = i * U + (u - lag)
            if isinstance(g, int) and not 0 <= g < GROUPS:
                return None
            return g, (u - lag) % 4, i * (U // 4) + (u - lag) // 4

        def ring_places_of(u, lag, j):
            place = eighth(u, lag) * T + j
            return (place, RING + place) if place < SPAN - 1 else (place,)

        def edge_bank(slot):
            return bank[(0, 1, 4, 5)[slot]]

        LAPS = [len(range(k, GROUPS, 4)) for k in range(4)]

        def eighth(u, lag):
            return (u - lag) % 8

        block = ctx.enter_context(nc.Block())

        def flag_of(eng):
            eng.wait_ge(S["flag_rdy"], 1)
            return eng.value_load(flag_i[0:1, 0:1], min_val=0, max_val=1 << 10)

        def ring_places(after):
            V = nc.vector
            after(V.tensor_scalar(offs[:, :], a_f[0:1, 0:TILES], float(D), None, ALU.mult))
            after(V.tensor_copy(offs_i[:, :], offs[:, :]))
            after(V.tensor_single_scalar(ring_at[:, :], offs_i[:, :], (RING - 1) * D, ALU.bitwise_and))

        def general_loads(sp, layer):
            table = (table0, table1)[layer]
            w = (W0, D)[layer]
            z = {n: S[f"z{layer}_{n}"] for n in ("zero", "init", "edge", "scat", "mvin", "mvout")}
            zeros, low, high = gath[:, 0, :, 0:w], gath[:, 1, :, 0:w], gath[:, 2, :, 0:w]
            sp.wait_ge(z["zero"], 1)
            sp.dma_start(table[2 * ROWS:, :], gath[:, 0, 0, 0:w]).then_inc(z["init"], 16)
            with sp.Fori(GROUPS, 2 * GROUPS) as g:
                sp.dma_start(rows4(table, g), zeros).then_inc(z["init"], 16)
            if layer == 0:
                sp.dma_start(z_edge[:, :], edgeT[:, 0:P]).then_inc(z["edge"], 16)
                with sp.Fori(1, TILES) as k:
                    sp.wait_ge(z["scat"], k * 16)
                    sp.dma_start(z_edge[:, :], edgeT[:, bass.ds(k * P, P)]).then_inc(z["edge"], 16)
            sp.wait_ge(z["scat"], 16 * TILES)

            def move(g):
                sp.dma_start(low, rows4(table, g)).then_inc(z["mvin"], 16)
                sp.dma_start(high, rows4(table, g + GROUPS)).then_inc(z["mvin"], 16)
                sp.wait_ge(z["mvin"], g * 32 + 32)
                sp.dma_start(rows4(table, g), high).then_inc(z["mvout"], 16)
                sp.dma_start(rows4(table, g + GROUPS), low).then_inc(z["mvout"], 16)

            move(0)
            with sp.Fori(1, GROUPS) as g:
                sp.wait_ge(z["mvout"], g * 32)
                move(g)
            sp.wait_ge(z["mvout"], 32 * GROUPS)

        def own_rows(sp, bad_n, n):
            first = n * (T * P) + (bad_n > 0) * ROWS
            return table0[bass.ds(first, T * P), :].rearrange("(j p) f -> p j f", p=P)

        def general_gathers(pool, layer):
            table = (table0, table1)[layer]
            w = (W0, D)[layer]
            z = {n: S[f"z{layer}_{n}"] for n in ("init", "idx", "src", "sum", "scat", "mvout", "carry")}
            pool.wait_ge(z["init"], 16 * (GROUPS + 1))

            def tile(k):
                pool.wait_ge(z["idx"], k + 1)
                nc.gpsimd.tensor_tensor(z_scr[:, 0:1], z_scr[:, 2:3], z_scr[:, 3:4], ALU.add).then_inc(
                    z["carry"], 1)
                pool.indirect_dma_start(
                    out=z_rows[:, 0:w], out_offset=None, in_=table[0:ROWS, :],
                    in_offset=bass.IndirectOffsetOnAxis(ap=z_src[:, :], axis=0),
                    bounds_check=ROWS - 1, oob_is_err=False).then_inc(z["src"], 16)
                pool.wait_ge(z["sum"], k + 1)
                nc.gpsimd.tensor_tensor(z_scr[:, 1:2], z_scr[:, 2:3], z_scr[:, 3:4], ALU.add).then_inc(
                    z["carry"], 1)
                pool.indirect_dma_start(
                    in_=z_sum[:, 0:w], in_offset=None, out=table[:, :],
                    out_offset=bass.IndirectOffsetOnAxis(ap=z_dst[:, :], axis=0),
                    bounds_check=2 * ROWS + P - 1, oob_is_err=True,
                    compute_op=ALU.add).then_inc(z["scat"], 16)

            with pool.Fori(0, TILES) as k:
                tile(k)
            pool.wait_ge(z["mvout"], 32 * GROUPS)
            if layer == 0:
                pool.wait_ge(S["z0_reset"], 1)

        def general_vector(dve, layer):
            V = nc.vector
            w = (W0, D)[layer]
            z = {n: S[f"z{layer}_{n}"] for n in ("zero", "idx", "src", "emm", "tgt", "same", "sum", "scat", "carry")}
            V.memset(gath[:, 0, :, 0:D], 0.0)
            V.memset(gath[:, 0, :, D:], 1.0)
            V.memset(z_scr[:, :], 0)
            V.memset(z_msg[:, D:], 0.0).then_inc(z["zero"], 1)

            def tile(k, first=False):
                if not first:
                    dve.wait_ge(z["scat"], k * 16)
                    dve.wait_ge(z["carry"], k * 2)
                V.tensor_copy(z_src[:, :], src_i[:, bass.ds(k, 1)])
                V.tensor_copy(z_node[:, :], dst_f[:, bass.ds(k, 1)].to_broadcast([P, P])).then_inc(z["idx"], 1)
                dve.wait_ge(z["emm"], k + 1)
                V.tensor_scalar(z_same[:, :], bank[5][:, 0:P], dst_f[:, bass.ds(k, 1)], None,
                                ALU.is_equal).then_inc(z["tgt"], 1)
                dve.wait_ge(z["src"], k * 16 + 16)
                if layer == 0:
                    V.tensor_tensor(z_pre[:, :], bank[7][:, 0:D], z_rows[:, 0:D], ALU.add)
                else:
                    V.tensor_copy(z_msg[:, 0:D], z_rows[:, 0:D])
                dve.wait_ge(z["tgt"], k * 5 + 1)
                V.tensor_tensor(z_dup[:, :], z_same[:, :], before[:, 0:P], ALU.mult).then_inc(z["tgt"], 1)
                dve.wait_ge(z["tgt"], k * 5 + 2)
                V.reduce_sum(z_cnt[:, 0:1], z_dup[:, :], AX)
                V.tensor_scalar(z_cnt[:, 1:2], dst_f[:, bass.ds(k, 1)], before[:, P:], -float(ROWS),
                                ALU.subtract, ALU.add).then_inc(z["tgt"], 1)
                dve.wait_ge(z["tgt"], k * 5 + 3)
                V.scalar_tensor_tensor(z_cnt[:, 2:3], z_cnt[:, 0:1], 0.0, z_cnt[:, 1:2],
                                       ALU.is_equal, ALU.mult).then_inc(z["tgt"], 1)
                dve.wait_ge(z["tgt"], k * 5 + 4)
                V.tensor_scalar(z_dst[:, :], z_cnt[:, 2:3], before[:, P:], 2.0 * ROWS, ALU.add,
                                ALU.add).then_inc(z["tgt"], 1)
                dve.wait_ge(z["same"], k + 1)
                dve.wait_ge(z["tgt"], k * 5 + 5)
                V.tensor_copy(z_sum[:, 0:w], bank[6][:, 0:w]).then_inc(z["sum"], 1)

            tile(0, True)
            with dve.Fori(1, TILES) as k:
                tile(k)
            dve.wait_ge(z["scat"], 16 * TILES)
            if layer == 0:
                count = [0]

                def after(ins):
                    count[0] += 1
                    ins.then_inc(S["z_chain"], 1)
                    dve.wait_ge(S["z_chain"], count[0])

                after(V.tensor_scalar(src_use[:, :], tile_base[:, 0:TILES], before[:, P:], None, ALU.add))
                after(V.tensor_scalar(a_f[:, 0:TILES], iota[:, 0:TILES], -1.0, 0.0, ALU.add, ALU.max))
                ring_places(after)
                after(V.tensor_tensor(badrow[:, 0, :], a_f[:, 0:TILES], iota[:, 0:TILES], ALU.subtract))
                after(V.tensor_scalar(badrow[:, 1, :], badrow[:, 0, :], float(P), None, ALU.mult))
                after(V.tensor_scalar(badrow[:, 0, :], badrow[:, 1, :], before[:, P:], None, ALU.add))
                for k in range(SPAN):
                    after(V.tensor_scalar(rel[:, :, k], badrow[:, 0, :], float(P * k), None, ALU.add))
                V.memset(we[:, :], 0.0)
                V.memset(bias4[:, 1, :, :], 0.0).then_inc(S["z0_reset"], 1)
                dve.wait_ge(S["z0_reset"], 1)

        def general_products(pe, layer):
            w = (W0, D)[layer]
            z = {n: S[f"z{layer}_{n}"] for n in ("idx", "edge", "emm", "tgt", "msg", "same")}

            def tile(k):
                pe.wait_ge(z["idx"], k + 1)
                if layer == 0:
                    pe.wait_ge(z["edge"], k * 16 + 16)
                    nc.tensor.matmul(bank[7][:, 0:D], ones3[:, :], bias4[:, 1, 0, :], start=True, stop=False)
                    nc.tensor.matmul(bank[7][:, 0:D], z_edge[:, :], we[:, :], start=False, stop=True)
                nc.tensor.transpose(bank[5][:, 0:P], z_node[:, :], ident[:, :]).then_inc(z["emm"], 1)
                if layer == 0:
                    pe.wait_ge(z["msg"], k + 1)
                pe.wait_ge(z["tgt"], k * 5 + 2)
                nc.tensor.matmul(bank[6][:, 0:w], z_same[:, :], z_msg[:, 0:w], start=True,
                                 stop=True).then_inc(z["same"], 1)

            with pe.Fori(0, TILES) as k:
                tile(k)
            if layer == 0:
                pe.wait_ge(S["z0_reset"], 1)

        def general_messages(act):
            z = {n: S[f"z0_{n}"] for n in ("tgt", "msg")}
            with act.Fori(0, TILES) as k:
                act.wait_ge(z["tgt"], k * 5 + 2)
                nc.scalar.activation(z_msg[:, 0:D], z_pre[:, :], ACT.Relu,
                                     scale=z_rows[:, D:]).then_inc(z["msg"], 1)

        @block.sync
        def _(sp):
            for dst, src in ((before, before_in), (ident, ident_in), (iota, iota_in), (tile_base, tile_base_in), (wn, w_node),
                             (we, w_edge), (group_tile, group_tile_in)):
                sp.dma_start(dst[:, :], src).then_inc(S["consts_in"], 16)
            sp.dma_start(tile_no[:, :, :], tile_no_in).then_inc(S["consts_in"], 16)
            sp.dma_start(w1[:, :, :], w_out.rearrange("(k p) f -> p k f", p=P)).then_inc(S["consts_in"], 16)
            for r in range(3):
                for k, b in enumerate((b_node, b_edge, root, b_out)):
                    sp.dma_start(brow[r:r + 1, k, :], b).then_inc(S["consts_in"], 16)
            for dst, src in ((src_i, srcT), (dst_i, dstT), (cur_i, dst_cur), (next_i, dst_next),
                             (first_i, dst_first)):
                sp.dma_start(dst[:, :], src).then_inc(S["idx_in"], 16)
            sp.dma_start(dst_rows_i[:, :, :], dst_rows).then_inc(S["idx_in"], 16)

            def load_nodes(i, u):
                g = grp(i, u, 0)
                if g:
                    g, slot, r = g
                    need(sp, S["n_h"], g - 7)
                    need(sp, S[f"x_in{slot}"], 16 * r)
                    sp.dma_start(xb[:, eighth(u, 0), :, :], rows4(x, g)).then_inc(S[f"x_in{slot}"], 16)

            rounds(sp, load_nodes, 0)

            for k in range(4):
                sp.wait_ge(S[f"t0_out{k}"], 16 * LAPS[k])

            bad_n = flag_of(sp)
            with sp.If(bad_n > 0):
                general_loads(sp, 0)

            def load_layer0(i, u):
                g = grp(i, u, 0)
                if g:
                    g, slot, r = g
                    need(sp, S["emm_done"], g - 3)
                    sp.dma_start(edge[:, slot, :], edgeT[:, bass.ds(g * (T * P), T * P)]).then_inc(
                        S[f"e_in{slot}"], 16)
                n = grp(i, u, 3)
                if n:
                    n, slot, r = n
                    need(sp, S["q_rdy"], n - 3)
                    sp.dma_start(ya[:, slot, :, :], own_rows(sp, bad_n, n)).then_inc(S[f"y_in{slot}"], 16)
                n = grp(i, u, 4)
                if n:
                    n, slot, r = n
                    need(sp, S["x1_rdy"], n - 3)
                    sp.dma_start(xb[:, slot, :, :], rows4(x, n)).then_inc(S[f"xl_in{slot}"], 16)

            sp.wait_ge(S["n_h"], GROUPS)
            rounds(sp, load_layer0, 4)

            for k in range(4):
                sp.wait_ge(S[f"x1_out{k}"], 16 * LAPS[k])
                sp.wait_ge(S[f"t1_out{k}"], 16 * LAPS[k])

            with sp.If(bad_n > 0):
                general_loads(sp, 1)

            def load_layer1(i, u):
                g = grp(i, u, 0)
                if g:
                    g, slot, r = g
                    need(sp, S["o_y"], g - 7)
                    need(sp, S[f"xx_in{slot}"], 16 * r)
                    sp.dma_start(xb[:, eighth(u, 0), :, :], rows4(x1_dram, g)).then_inc(S[f"xx_in{slot}"], 16)

            sp.wait_ge(S["x1_rdy"], GROUPS)
            rounds(sp, load_layer1, 0)

        @block.gpsimd
        def _(pool):
            def gather(dst, table, col, landed):
                pool.indirect_dma_start(
                    out=dst, out_offset=None, in_=table,
                    in_offset=bass.IndirectOffsetOnAxis(ap=col, axis=0),
                    bounds_check=ROWS - 1, oob_is_err=False).then_inc(landed, 16)

            for k in range(4):
                pool.wait_ge(S[f"t0_out{k}"], 16 * LAPS[k])

            bad_n = flag_of(pool)
            with pool.If(bad_n > 0):
                general_gathers(pool, 0)

            def place_indices(g, slot):
                nc.gpsimd.tensor_copy(idx[:, slot, :], src_use[:, bass.ds(g * T, T)]).then_inc(
                    S["idx_rdy"], 1)

            def fetch0(i, u):
                g = grp(i, u, 0)
                if g:
                    g, slot, r = g
                    pool.wait_ge(S["idx_rdy"], g + 1)
                    need(pool, S["msg_rdy"], g - 3)
                    n = grp(i, u, -1)
                    if n:
                        need(pool, S[f"g_in{n[1]}"], 64 * n[2])
                        place_indices(*n[:2])
                    for j in range(T):
                        gather(gath[:, slot, j, :], table0[0:ROWS, :], idx[:, slot, j:j + 1], S[f"g_in{slot}"])

            place_indices(0, 0)
            rounds(pool, fetch0, 0)

            for k in range(4):
                pool.wait_ge(S[f"t1_out{k}"], 16 * LAPS[k])
                pool.wait_ge(S[f"g_in{k}"], 64 * LAPS[k])
            pool.wait_ge(S["seg_done"], GROUPS)

            with pool.If(bad_n > 0):
                general_gathers(pool, 1)

            def fetch1(i, u):
                g = grp(i, u, 0)
                if g:
                    g, slot, r = g
                    pool.wait_ge(S["idx_rdy"], GROUPS + g + 1)
                    need(pool, S["o_seg"], g - 5)
                    n = grp(i, u, -1)
                    if n:
                        need(pool, S[f"r_in{n[1]}"], 64 * n[2])
                        place_indices(*n[:2])
                    for j in range(T):
                        gather(ring[:, eighth(u, 0) * T + j, :], table1[0:ROWS, :], idx[:, slot, j:j + 1],
                               S[f"r_in{slot}"])

            place_indices(0, 0)
            rounds(pool, fetch1, 0)

        @block.vector
        def _(dve):
            chain = [0]

            def link(ins):
                chain[0] += 1
                ins.then_inc(S["setup"], 1)
                dve.wait_ge(S["setup"], chain[0])

            V = nc.vector
            link(V.memset(ones3[:, :], 1.0))
            link(V.memset(eps_t[:, :], EPS))
            V.memset(ones[:, :], 1.0).then_inc(S["ones_rdy"], 1)
            dve.wait_ge(S["consts_in"], 16 * 21)
            dve.wait_ge(S["idx_in"], 16 * 6)
            link(V.tensor_copy(count4[:, :, :], iota[:, 0:TILES].unsqueeze(2).to_broadcast([P, TILES, T])))
            for k, ids in enumerate((src_i, dst_i)):
                link(V.tensor_single_scalar(part_i[:, :], ids[:, :], P - 1, ALU.bitwise_and))
                link(V.tensor_copy(digits[:, 2 * k, :], part_i[:, :]))
                link(V.tensor_single_scalar(part_i[:, :], ids[:, :], 7, ALU.logical_shift_right))
                link(V.tensor_copy(digits[:, 2 * k + 1, :], part_i[:, :]))
            link(V.tensor_copy(dst_f[:, :], dst_i[:, :]))
            link(V.tensor_copy(src_use[:, :], src_i[:, :]))
            link(V.tensor_copy(first_f[:, :], first_i[:, :]))
            for c in range(4):
                ins = V.tensor_scalar(cmp[0:TILES // 4, c, :], tile_base[0:TILES // 4, 0:TILES + 1],
                                      first_f[:, c:c + 1], None, ALU.is_gt)
            ins.then_inc(S["cmp_rdy"], 1)
            link(V.tensor_copy(cur_f[:, :], cur_i[:, :]))
            link(V.tensor_copy(next_f[:, :], next_i[:, :]))
            link(V.tensor_tensor(badrow[:, 0, :], cur_f[:, :], next_f[:, :], ALU.is_gt))
            link(V.reduce_max(bad[:, 0:1], badrow[:, 0, :], AX))
            dve.wait_ge(S["a_psum"], 1)
            link(V.tensor_scalar(a_f[:, :], bank[0][:, 0:TILES + 1], -1.0, 0.0, ALU.add, ALU.max))
            ring_places(link)
            link(V.tensor_copy(dst_rows_f[:, :, :], dst_rows_i[:, :, :]))
            for k in range(SPAN):
                if k:
                    dve.wait_ge(S["rel_psum"], k)
                for c in range(4):
                    ins = V.tensor_scalar(chosen[:, c, :], a_f[0:TILES // 4, 0:TILES], tile_no[:, k, c:c + 1],
                                          None, ALU.is_equal)
                ins.then_inc(S["chosen_rdy"], 1)
            dve.wait_ge(S["rel_psum"], SPAN)
            for k in range(SPAN):
                ins = V.tensor_tensor(rel[:, :, k], bank[4 + k][:, 0:TILES], tile_base[:, 0:TILES],
                                      ALU.subtract)
            link(ins)
            link(V.tensor_tensor(badrow[:, 0, :], a_f[:, 1:TILES + 1], a_f[:, 0:TILES], ALU.subtract))
            link(V.tensor_scalar(badrow[:, 0, :], badrow[:, 0, :], SPAN - 1.0, None, ALU.is_gt))
            link(V.reduce_max(bad[:, 1:2], badrow[:, 0, :], AX))
            link(V.tensor_tensor(badrow[:, 0, :], a_f[:, 0:TILES], group_tile[:, :], ALU.subtract))
            link(V.tensor_scalar(badrow[:, 1, :], badrow[:, 0, :], -float(BACK), None, ALU.is_lt))
            link(V.reduce_max(bad[:, 2:3], badrow[:, 1, :], AX))
            link(V.tensor_scalar(badrow[:, 1, :], badrow[:, 0, :], float(AHEAD), None, ALU.is_gt))
            link(V.reduce_max(bad[:, 3:4], badrow[:, 1, :], AX))
            V.reduce_sum(bad[:, 4:5], bad[:, 0:4], AX).then_inc(S["bad_psum"], 1)

            link(V.tensor_tensor(bsum[:, 0, :], brow[:, 0, :], brow[:, 2, :], ALU.add))
            link(V.tensor_tensor(bsum[:, 1, :], brow[:, 1, :], brow[:, 2, :], ALU.subtract))
            link(V.tensor_copy(bsum[:, 2, :], brow[:, 3, :]))
            link(V.tensor_copy(bpart[:, 0, :, :], bsum[:, :, :]))
            link(V.tensor_tensor(bres[:, :, :], bsum[:, :, :], bpart[:, 0, :, :], ALU.subtract))
            link(V.tensor_copy(bpart[:, 1, :, :], bres[:, :, :]))
            link(V.tensor_tensor(bres[:, :, :], bres[:, :, :], bpart[:, 1, :, :], ALU.subtract))
            link(V.tensor_copy(bpart[:, 2, :, :], bres[:, :, :]))
            link(V.tensor_scalar(bsel[:, :, :], bpart[:, 0, :, :], ident[0:3, 0:1], None, ALU.mult))
            link(V.scalar_tensor_tensor(bsel[:, :, :], bpart[:, 1, :, :], ident[0:3, 1:2], bsel[:, :, :],
                                        ALU.mult, ALU.add))
            link(V.scalar_tensor_tensor(bsel[:, :, :], bpart[:, 2, :, :], ident[0:3, 2:3], bsel[:, :, :],
                                        ALU.mult, ALU.add))
            for j in range(T):
                ins = V.tensor_copy(bias4[:, :, j, :], bsel[:, :, :])
            link(ins)
            dve.wait_ge(S["bad_psum"], 2)
            V.tensor_copy(flag_i[0:1, 0:1], bank[1][0:1, 0:1]).then_inc(S["flag_rdy"], 1)

            def one_hots(n, k):
                g, slot, r = n
                need(dve, S["hist_done"], g + (k * GROUPS - 1))
                at = bass.ds(g * T, T)
                for hot, part, size in ((low_hot, 2 * k, P), (high_hot, 2 * k + 1, TILES)):
                    ins = V.tensor_tensor(hot[:, slot % 2, :, :], count4[:, 0:size, :],
                                          digits[:, part, at].unsqueeze(1).to_broadcast([P, size, T]),
                                          ALU.is_equal)
                ins.then_inc(S["hot_rdy"], 1)

            def send_step(i, u):
                g = grp(i, u, 0)
                if g:
                    one_hots(g, 0)

            rounds(dve, send_step, 0)
            dve.wait_ge(S["hist_done"], GROUPS)
            V.tensor_scalar(deg[:, 0, :], bank[2][:, 0:TILES], 1.0, None, ALU.add).then_inc(S["deg_sum"], 1)
            dve.wait_ge(S["deg_sqrt"], 1)
            V.reciprocal(c_send[:, :], dsq[:, 0, :]).then_inc(S["tables_rdy"], 1)
            dve.wait_ge(S["tables_rdy"], 1)

            def node_step(i, u):
                now = grp(i, u, 0)
                if now:
                    g, slot, r = now
                    dve.wait_ge(S[f"x_in{slot}"], 16 * (r + 1))
                    for j in range(T):
                        ins = V.bn_stats(bnst[:, slot % 2, j, :], xb[:, eighth(u, 0), j, :])
                    ins.then_inc(S["n_bn"], 1)
                last = grp(i, u, 1)
                if last:
                    m, mslot, mr = last
                    dve.wait_ge(S["n_sd"], m + 1)
                    V.reciprocal(rs[:, mslot, :], sd[:, mslot, :]).then_inc(S["n_rs"], 1)
                if now:
                    dve.wait_ge(S["n_bn"], g + 1)
                    need(dve, S["n_h"], g - 3)
                    one_hots(now, 1)
                if last:
                    dve.wait_ge(S["n_rs"], m + 1)
                    V.scalar_tensor_tensor(nb[:, mslot, :], mv[:, mslot, :, 0], -1.0, rs[:, mslot, :],
                                           ALU.mult, ALU.mult).then_inc(S["n_coef"], 1)
                c = grp(i, u, 5)
                if c:
                    need(dve, S[f"t0_out{c[1]}"], 16 * c[2])
                    V.tensor_copy(ya[:, c[1], :, D], c_send[:, bass.ds(c[0] * T, T)]).then_inc(S["n_col"], 1)
                if now:
                    for j in range(T):
                        ins = V.bn_aggr(mv[:, slot, j, :], bnst[:, slot % 2, j, :])
                    ins.then_inc(S["n_stats"], 1)

            rounds(dve, node_step, 5)
            dve.wait_ge(S["hist_done"], 2 * GROUPS)
            V.tensor_scalar(deg[:, 1, :], bank[3][:, 0:TILES], 1.0, None, ALU.add)
            V.tensor_scalar(deg[:, 2, :], bank[3][:, 0:TILES], 1.0, None, ALU.max).then_inc(S["deg_sum"], 1)
            dve.wait_ge(S["deg_sum"], 2)
            V.reciprocal(rinv[:, :], deg[:, 1, :])
            dve.wait_ge(S["deg_sqrt"], 2)
            V.reciprocal(rn[:, :], dsq[:, 1, :])
            V.reciprocal(norm1[:, :], dsq[:, 2, :]).then_inc(S["tables_rdy"], 1)
            dve.wait_ge(S["tables_rdy"], 2)

            def picks(n, par, ready):
                at = bass.ds(n * T, T)
                V.tensor_tensor(pick[:, par, :, :],
                                iota[:, 0:P].unsqueeze(1).to_broadcast([P, T * SPAN, P]),
                                rel[:, at, :].rearrange("p t w -> p (t w)").unsqueeze(2).to_broadcast(
                                    [P, T * SPAN, P]),
                                ALU.is_equal).then_inc(ready, 1)

            for k in range(4):
                dve.wait_ge(S[f"t0_out{k}"], 16 * LAPS[k])
            bad_n = flag_of(dve)
            with dve.If(bad_n > 0):
                general_vector(dve, 0)

            def layer0_step(i, u):
                last = grp(i, u, LAG + 2)
                if last:
                    m, mslot, mr = last
                    dve.wait_ge(S["l_bn"], m + 1)
                now = grp(i, u, LAG + 1)
                if now:
                    n, slot, r = now
                    dve.wait_ge(S["seg_done"], n + 1)
                    dve.wait_ge(S["q_rdy"], n + 1)
                    for j in range(T):
                        ins = V.scalar_tensor_tensor(v[:, j, :], bank[2 + slot % 2][:, j * D:(j + 1) * D],
                                                     rn[:, bass.ds(n * T + j, 1)], q[:, slot % 2, j, :],
                                                     ALU.mult, ALU.add)
                    ins.then_inc(S["v_rdy"], 1)
                if last:
                    for j in range(T):
                        ins = V.bn_aggr(mv[:, mslot, j, :], bnst[:, mslot % 2, j, :])
                    ins.then_inc(S["l_stats"], 1)
                if now:
                    dve.wait_ge(S["v_rdy"], n + 1)
                    dve.wait_ge(S[f"xl_in{slot}"], 16 * (r + 1))
                    need(dve, S[f"x1_out{slot}"], 16 * r)
                    V.scalar_tensor_tensor(x1[:, slot, :, :], v[:, :, :], 0.0, xb[:, slot, :, :],
                                           ALU.max, ALU.add).then_inc(S["x1_rdy"], 1)
                if last:
                    at = bass.ds(m * T, T)
                    dve.wait_ge(S["l_sd"], m + 1)
                    V.reciprocal(rstd1[:, at], sd[:, mslot, :]).then_inc(S["l_rs"], 1)
                p = grp(i, u, LAG - 1)
                if p:
                    need(dve, S["seg_done"], p[0] - 1)
                    picks(p[0], p[1] % 2, S["pick_rdy"])
                if last:
                    dve.wait_ge(S["l_rs"], m + 1)
                    V.scalar_tensor_tensor(nb1[:, at], mv[:, mslot, :, 0], -1.0, rstd1[:, at],
                                           ALU.mult, ALU.mult).then_inc(S["l_nb"], 1)
                    V.tensor_tensor(sc1[:, mslot, :], rstd1[:, at], norm1[:, at], ALU.mult)
                if now:
                    dve.wait_ge(S["x1_rdy"], n + 1)
                    for j in range(T):
                        ins = V.bn_stats(bnst[:, slot % 2, j, :], x1[:, slot, j, :])
                    ins.then_inc(S["l_bn"], 1)
                if last:
                    dve.wait_ge(S["l_nb"], m + 1)
                    V.tensor_tensor(bi1[:, mslot, :], nb1[:, at], norm1[:, at], ALU.mult).then_inc(
                        S["l_coef"], 1)

            rounds(dve, layer0_step, LAG + 2)

            def layer1_step(i, u):
                n = grp(i, u, 0)
                if n:
                    n, slot, r = n
                    need(dve, S["o_seg"], n - 1)
                    picks(n, slot % 2, S["o_pick"])
                n = grp(i, u, 4)
                if n:
                    n, slot, r = n
                    dve.wait_ge(S["o_tp"], n + 1)
                    need(dve, S["o_mm"], n - 1)
                    V.tensor_copy(hT[:, slot % 2, :], bank[6 + slot % 2][:, :]).then_inc(S["o_hT"], 1)
                n = grp(i, u, 6)
                if n:
                    n, slot, r = n
                    dve.wait_ge(S["o_nrm"], n + 1)
                    V.reciprocal(inv[:, slot, :], nrm[:, slot, :]).then_inc(S["o_inv"], 1)
                    dve.wait_ge(S["o_inv"], n + 1)
                    need(dve, S[f"y_out{slot}"], 16 * r)
                    for j in range(T):
                        ins = V.scalar_tensor_tensor(x1[:, slot, j, :], bank[2 + slot % 2][:, j * D:(j + 1) * D],
                                                     inv[:, slot, j:j + 1], xb[:, eighth(u, 6), j, :], ALU.mult, ALU.add)
                    ins.then_inc(S["o_y"], 1)

            for k in range(4):
                dve.wait_ge(S[f"x1_out{k}"], 16 * LAPS[k])
                dve.wait_ge(S[f"t1_out{k}"], 16 * LAPS[k])
            with dve.If(bad_n > 0):
                general_vector(dve, 1)
            rounds(dve, layer1_step, 7)

        @block.tensor
        def _(pe):
            mm = nc.tensor.matmul
            pe.wait_ge(S["consts_in"], 16 * 21)
            pe.wait_ge(S["cmp_rdy"], 1)
            pe.wait_ge(S["ones_rdy"], 1)
            K = TILES // 4
            for c in range(4):
                ins = mm(bank[0][:, 0:TILES + 1], ones[0:K, :], cmp[0:K, c, :], start=c == 0, stop=c == 3)
            ins.then_inc(S["a_psum"], 1)
            for k in range(SPAN):
                pe.wait_ge(S["chosen_rdy"], k + 1)
                for c in range(4):
                    ins = mm(bank[4 + k][:, 0:TILES], dst_rows_f[:, c, :], chosen[:, c, :], start=c == 0,
                             stop=c == 3)
                ins.then_inc(S["rel_psum"], 1)
            pe.wait_ge(S["bad_psum"], 1)
            mm(bank[1][:, 0:1], ones[:, :], bad[:, 4:5], start=True, stop=True).then_inc(S["bad_psum"], 1)

            def histogram(n, k):
                g, slot, r = n
                pe.wait_ge(S["hot_rdy"], g + (k * GROUPS + 1))
                for j in range(T):
                    ins = mm(bank[2 + k][:, 0:TILES], low_hot[:, slot % 2, :, j], high_hot[:, slot % 2, :, j],
                             start=isinstance(g, int) and g == 0 and j == 0,
                             stop=isinstance(g, int) and g == GROUPS - 1 and j == T - 1,
                             skip_group_check=True)
                ins.then_inc(S["hist_done"], 1)

            def send_step(i, u):
                g = grp(i, u, 0)
                if g:
                    histogram(g, 0)

            rounds(pe, send_step, 0)

            def node_step(i, u):
                g = grp(i, u, 3)
                if g:
                    g, slot, r = g
                    pe.wait_ge(S["n_h"], g + 1)
                    need(pe, S["n_hT"], g - 1)
                    for j in range(T):
                        ins = nc.tensor.transpose(bank[4 + slot % 2][:, j * P:(j + 1) * P], h[:, slot, j, :],
                                                  ident[:, :])
                    ins.then_inc(S["n_tp"], 1)
                g = grp(i, u, 5)
                if g:
                    g, slot, r = g
                    pe.wait_ge(S["n_hT"], g + 1)
                    need(pe, S["n_evac"], g - 1)
                    affine(bank[6 + slot % 2], 0, [(hT[:, slot % 2, :], wn[:, :])], S["n_mm"])
                g = grp(i, u, 0)
                if g:
                    histogram(g, 1)

            def affine(out_bank, b, pairs, done):
                mm(out_bank[:, :], ones3[:, :], bias4[:, b, :, :].rearrange("k j f -> k (j f)"),
                   start=True, stop=False, skip_group_check=True)
                for j in range(T):
                    for rows, w in pairs:
                        ins = mm(out_bank[:, j * D:(j + 1) * D], rows[:, j * P:(j + 1) * P], w,
                                 start=False, stop=True, skip_group_check=True)
                ins.then_inc(done, 1)

            pe.wait_ge(S["flag_rdy"], 1)
            rounds(pe, node_step, 5)

            def places(n):
                return nc.values_load_multi_w_load_instructions(
                    ring_at[0:1, bass.ds(n * T, T)], engines=(pe.engine,), min_val=0,
                    max_val=(RING - 1) * D)[1]

            def sums(place, par, out_bank, done):
                for j in range(T):
                    for k in range(SPAN):
                        ins = mm(out_bank[:, j * D:(j + 1) * D], pick[:, par, j * SPAN + k, :],
                                 ring_flat[:, k * D:][:, bass.ds(place[j], D)],
                                 start=k == 0, stop=k == SPAN - 1)
                ins.then_inc(done, 1)

            def layer0_step(i, u):
                n = grp(i, u, LAG)
                if n:
                    place = places(n[0])
                g = grp(i, u, 0)
                if g:
                    g, slot, r = g
                    pe.wait_ge(S[f"e_in{slot}"], 16 * (r + 1))
                    need(pe, S["msg_rdy"], g - 3)
                    affine(edge_bank(slot), 1, [(edge[:, slot, :], we[:, :])], S["emm_done"])
                g = grp(i, u, 1)
                if g:
                    g, slot, r = g
                    pe.wait_ge(S[f"g_in{slot}"], 64 * (r + 1))
                    mm(edge_bank(slot)[:, :], ident[:, :], gath[:, slot, :, 0:D], start=False, stop=True,
                       skip_group_check=True).then_inc(S["sum_rdy"], 1)
                if n:
                    n, slot, r = n
                    pe.wait_ge(S["pick_rdy"], n + 1)
                    if isinstance(n, int):
                        pe.wait_ge(S["msg_rdy"], min(n + 4, GROUPS))
                    else:
                        pe.wait_ge(S["msg_rdy"], n + 4)
                    need(pe, S["v_rdy"], n - 1)
                    sums(place, slot % 2, bank[2 + slot % 2], S["seg_done"])

            pe.wait_ge(S["tables_rdy"], 2)
            pe.wait_ge(S["n_hT"], GROUPS)
            bad_n = flag_of(pe)
            with pe.If(bad_n > 0):
                pe.wait_ge(S["n_evac"], GROUPS)
                general_products(pe, 0)
            rounds(pe, layer0_step, LAG)

            def layer1_step(i, u):
                m = grp(i, u, 1)
                if m:
                    place = places(m[0])
                n = grp(i, u, 5)
                if n:
                    n, slot, r = n
                    pe.wait_ge(S["o_hT"], n + 1)
                    pe.wait_ge(S["o_aT"], n + 1)
                    need(pe, S["o_y"], n - 1)
                    affine(bank[2 + slot % 2], 2, [(hT[:, slot % 2, :], w1[:, 0, :]),
                                                   (aT[:, slot % 2, :], w1[:, 1, :])], S["o_mm"])
                n = grp(i, u, 3)
                if n:
                    n, slot, r = n
                    pe.wait_ge(S["o_h"], n + 1)
                    pe.wait_ge(S["o_agg"], n + 1)
                    need(pe, S["o_hT"], n - 1)
                    need(pe, S["o_aT"], n - 1)
                    for j in range(T):
                        nc.tensor.transpose(bank[6 + slot % 2][:, j * P:(j + 1) * P], h[:, slot, j, :],
                                            ident[:, :])
                        ins = nc.tensor.transpose(bank[slot % 2][:, j * P:(j + 1) * P],
                                                  agg[:, slot % 2, j, :], ident[:, :])
                    ins.then_inc(S["o_tp"], 1)
                if m:
                    n, slot, r = m
                    pe.wait_ge(S["o_pick"], n + 1)
                    if isinstance(n, int) and n == 0:
                        for k in range(3):
                            pe.wait_ge(S[f"r_in{k}"], 64)
                    if not (isinstance(n, int) and n + 3 >= GROUPS):
                        pe.wait_ge(S[f"r_in{(slot + 3) % 4}"], 64 * (r + (slot + 3) // 4 + 1))
                    if isinstance(n, int):
                        pe.wait_ge(S["o_again"], min(n + 3, GROUPS - 1) // 8 + 1)
                    elif eighth(u, 1 - 3) == 0:
                        pe.wait_ge(S["o_again"], i + (u - 1 + 3) // 8 + 1)
                    need(pe, S["o_agg"], n - 1)
                    sums(place, slot % 2, bank[4 + slot % 2], S["o_seg"])

            pe.wait_ge(S["v_rdy"], GROUPS)
            pe.wait_ge(S["n_evac"], GROUPS)
            with pe.If(bad_n > 0):
                general_products(pe, 1)
            rounds(pe, layer1_step, 6)

        @block.scalar
        def _(act):
            A = nc.scalar.activation
            act.wait_ge(S["deg_sum"], 1)
            A(dsq[:, 0, :], deg[:, 0, :], ACT.Sqrt).then_inc(S["deg_sqrt"], 1)

            def node_step(i, u):
                g = grp(i, u, 1)
                if g:
                    g, slot, r = g
                    act.wait_ge(S["n_stats"], g + 1)
                    A(sd[:, slot, :], mv[:, slot, :, 1], ACT.Sqrt, bias=eps_t[:, :]).then_inc(S["n_sd"], 1)
                g = grp(i, u, 6)
                if g:
                    g, slot, r = g
                    act.wait_ge(S["n_mm"], g + 1)
                    need(act, S[f"t0_out{slot}"], 16 * r)
                    A(ya[:, slot, :, 0:D], bank[6 + slot % 2][:, :].rearrange("p (j f) -> p j f", f=D),
                      ACT.Copy).then_inc(S["n_evac"], 1)
                g = grp(i, u, 4)
                if g:
                    g, slot, r = g
                    act.wait_ge(S["n_tp"], g + 1)
                    need(act, S["n_mm"], g - 1)
                    A(hT[:, slot % 2, :], bank[4 + slot % 2][:, :], ACT.Copy).then_inc(S["n_hT"], 1)
                g = grp(i, u, 2)
                if g:
                    g, slot, r = g
                    act.wait_ge(S["n_coef"], g + 1)
                    need(act, S["n_tp"], g - 3)
                    for j in range(T):
                        ins = A(h[:, slot, j, :], xb[:, eighth(u, 2), j, :], ACT.Relu,
                                bias=nb[:, slot, j:j + 1], scale=rs[:, slot, j:j + 1])
                    ins.then_inc(S["n_h"], 1)
                g = grp(i, u, 6)
                if g:
                    g, slot, r = g
                    act.wait_ge(S["n_evac"], g + 1)
                    act.wait_ge(S["n_col"], g + 1)
                    act.dma_start(rows4(table0, g), ya[:, slot, :, :]).then_inc(S[f"t0_out{slot}"], 16)

            rounds(act, node_step, 6)
            act.wait_ge(S["deg_sum"], 2)
            A(dsq[:, 1:3, :], deg[:, 1:3, :], ACT.Sqrt).then_inc(S["deg_sqrt"], 1)

            def layer0_step(i, u):
                g = grp(i, u, 1)
                if g:
                    g, slot, r = g
                    act.wait_ge(S["sum_rdy"], g + 1)
                    need(act, S["seg_done"], g - 5)
                    for j in range(T):
                        for place in ring_places_of(u, 1, j):
                            ins = A(ring[:, place, :], edge_bank(slot)[:, j * D:(j + 1) * D], ACT.Relu,
                                    scale=gath[:, slot, j, D:D + 1])
                    ins.then_inc(S["msg_rdy"], 1)
                n = grp(i, u, LAG + 2)
                if n:
                    n, slot, r = n
                    act.wait_ge(S["l_stats"], n + 1)
                    A(sd[:, slot, :], mv[:, slot, :, 1], ACT.Sqrt, bias=eps_t[:, :]).then_inc(S["l_sd"], 1)
                    act.wait_ge(S["x1_rdy"], n + 1)
                    act.dma_start(rows4(x1_dram, n), x1[:, slot, :, :]).then_inc(S[f"x1_out{slot}"], 16)
                n = grp(i, u, LAG)
                if n:
                    n, slot, r = n
                    act.wait_ge(S[f"y_in{slot}"], 16 * (r + 1))
                    need(act, S["v_rdy"], n - 1)
                    for j in range(T):
                        ins = A(q[:, slot % 2, j, :], ya[:, slot, j, 0:D], ACT.Relu,
                                scale=rinv[:, bass.ds(n * T + j, 1)])
                    ins.then_inc(S["q_rdy"], 1)
                n = grp(i, u, LAG + 3)
                if n:
                    n, slot, r = n
                    act.wait_ge(S["l_coef"], n + 1)
                    need(act, S[f"t1_out{slot}"], 16 * r)
                    for j in range(T):
                        ins = A(h[:, slot, j, :], x1[:, slot, j, :], ACT.Relu, bias=bi1[:, slot, j:j + 1],
                                scale=sc1[:, slot, j:j + 1])
                    ins.then_inc(S["t1_rdy"], 1)
                    act.wait_ge(S["t1_rdy"], n + 1)
                    act.dma_start(rows4(table1, n), h[:, slot, :, :]).then_inc(S[f"t1_out{slot}"], 16)

            act.wait_ge(S["tables_rdy"], 2)
            act.wait_ge(S["n_tp"], GROUPS)
            bad_n = flag_of(act)
            with act.If(bad_n > 0):
                general_messages(act)
            rounds(act, layer0_step, LAG + 3)

            def repeat_first(r_in, value):
                act.wait_ge(r_in, value)
                A(ring[:, RING:, :], ring[:, 0:SPAN - 1, :], ACT.Copy).then_inc(S["o_again"], 1)

            def layer1_step(i, u):
                g = grp(i, u, -3)
                if g and eighth(u, -3) == 0:
                    g, slot, r = g
                    repeat_first(S[f"r_in{slot}"], 64 * (r + 1))
                n = grp(i, u, 6)
                if n:
                    n, slot, r = n
                    act.wait_ge(S["o_mm"], n + 1)
                    need(act, S["o_inv"], n - 3)
                    for j in range(T):
                        ins = A(junk[:, j, :], bank[2 + slot % 2][:, j * D:(j + 1) * D], ACT.Square,
                                accum_out=ss[:, slot, j:j + 1])
                    ins.then_inc(S["o_sq"], 1)
                    act.wait_ge(S["o_sq"], n + 1)
                    A(nrm[:, slot, :], ss[:, slot, :], ACT.Sqrt).then_inc(S["o_nrm"], 1)
                n = grp(i, u, 2)
                if n:
                    n, slot, r = n
                    act.wait_ge(S["o_seg"], n + 1)
                    need(act, S["o_tp"], n - 1)
                    for j in range(T):
                        ins = A(agg[:, slot % 2, j, :], bank[4 + slot % 2][:, j * D:(j + 1) * D], ACT.Copy,
                                scale=norm1[:, bass.ds(n * T + j, 1)])
                    ins.then_inc(S["o_agg"], 1)
                    act.wait_ge(S[f"xx_in{slot}"], 16 * (r + 1))
                    for j in range(T):
                        ins = A(h[:, slot, j, :], xb[:, eighth(u, 2), j, :], ACT.Relu,
                                bias=nb1[:, bass.ds(n * T + j, 1)], scale=rstd1[:, bass.ds(n * T + j, 1)])
                    ins.then_inc(S["o_h"], 1)
                n = grp(i, u, 4)
                if n:
                    n, slot, r = n
                    act.wait_ge(S["o_tp"], n + 1)
                    need(act, S["o_mm"], n - 1)
                    A(aT[:, slot % 2, :], bank[slot % 2][:, :], ACT.Copy).then_inc(S["o_aT"], 1)
                n = grp(i, u, 7)
                if n:
                    n, slot, r = n
                    act.wait_ge(S["o_y"], n + 1)
                    act.dma_start(rows4(out, n), x1[:, slot, :, :]).then_inc(S[f"y_out{slot}"], 16)

            for k in range(4):
                act.wait_ge(S[f"x1_out{k}"], 16 * LAPS[k])
                act.wait_ge(S[f"t1_out{k}"], 16 * LAPS[k])
            repeat_first(S["r_in0"], 64)
            rounds(act, layer1_step, 7)
            for k in range(4):
                act.wait_ge(S[f"y_out{k}"], 16 * LAPS[k])


def kernel(x, src, dst, edge_attr_128, L0_gnn_W_node, L0_gnn_b_node, L0_gnn_W_edge, L0_gnn_b_edge,
           L0_gnn_root_emb, L1_gnn_weight, L1_gnn_bias):
    import numpy as np
    import concourse.bacc as bacc
    from concourse.bass_utils import run_bass_kernel_spmd

    pad = np.arange(NODES, ROWS, dtype=np.int32)
    zero_rows = np.zeros((ROWS - NODES, D), np.float32)
    src_all = np.concatenate([np.asarray(src), pad])
    dst_all = np.concatenate([np.asarray(dst), pad])
    dst_tiles = dst_all.reshape(TILES, P)
    edges = np.concatenate([np.asarray(edge_attr_128), zero_rows])
    tiles = np.arange(TILES + 4, dtype=np.float32)

    def across(row):
        return np.ascontiguousarray(np.broadcast_to(row, (P, row.shape[-1])))

    arrays = {
        "x": np.concatenate([np.asarray(x), zero_rows]),
        "edgeT": np.ascontiguousarray(edges.T),
        "srcT": np.ascontiguousarray(src_all.reshape(TILES, P).T),
        "dstT": np.ascontiguousarray(dst_tiles.T),
        "dst_cur": dst_all.reshape(P, TILES),
        "dst_next": np.concatenate([dst_all[1:], dst_all[-1:]]).reshape(P, TILES),
        "dst_first": np.ascontiguousarray(dst_tiles[:, 0]).reshape(TILES // 4, 4),
        "group_tile": across(np.float32(T) * np.arange(GROUPS, dtype=np.float32).repeat(T)),
        "tile_no": np.arange(TILES, dtype=np.float32).reshape(TILES // 4, 1, 4)
        - np.arange(SPAN, dtype=np.float32).reshape(1, SPAN, 1),
        "dst_rows": dst_all.reshape(TILES // 4, 4, P),
        "w_node": np.asarray(L0_gnn_W_node), "b_node": np.asarray(L0_gnn_b_node).reshape(1, D),
        "w_edge": np.asarray(L0_gnn_W_edge), "b_edge": np.asarray(L0_gnn_b_edge).reshape(1, D),
        "root": np.asarray(L0_gnn_root_emb), "w_out": np.asarray(L1_gnn_weight),
        "b_out": np.asarray(L1_gnn_bias).reshape(1, D),
        "ident": np.eye(P, dtype=np.float32),
        "iota": across(tiles),
        "tile_base": across(np.float32(P) * tiles),
        "before": np.concatenate([np.tri(P, k=-1, dtype=np.float32),
                                  np.arange(P, dtype=np.float32).reshape(P, 1)], 1),
    }
    nc = bacc.Bacc("TRN2", target_bir_lowering=False, num_devices=1)
    aps = [nc.dram_tensor(f"in_{k}", a.shape, mybir.dt.from_np(a.dtype), kind="ExternalInput").ap()
           for k, a in arrays.items()]
    out = nc.dram_tensor("out", (ROWS, D), mybir.dt.float32, kind="ExternalOutput").ap()
    gnn_kernel(nc, *aps, out)
    r = run_bass_kernel_spmd(nc, [{f"in_{k}": a for k, a in arrays.items()}], core_ids=[0])
    return r.results[0]["out"][:NODES]
```

```python
import concourse.bass as bass
from concourse import mybir
from contextlib import ExitStack


P = 128
D = 128
NODES = 50000
T = 4
GROUPS = -(-NODES // (P * T))
TILES = GROUPS * T
ROWS = TILES * P
RING = 32
SPAN = 3
REACH = 3
LAG = REACH + 1
LOW = 256
HIGH = ROWS // LOW
BACK, AHEAD = 8, REACH * T - SPAN
U = 8
PEEL = 2
EPS = 1e-5
W0 = D + 1


def gnn_kernel(nc: bass.Bass, x, edgeT, srcT, dstT, dst_cur, dst_next, dst_first, group_tile_in, tile_no_in,
               dst_rows_in, w_node, b_node, w_edge, b_edge, root, w_out, b_out, ident_in, iota_in,
               tile_base_in, before_in, out):
    f32, bf16, f16, i32 = mybir.dt.float32, mybir.dt.bfloat16, mybir.dt.float16, mybir.dt.int32
    ALU = mybir.AluOpType
    ACT = mybir.ActivationFunctionType
    AX = mybir.AxisListType.X

    table0 = nc.dram_tensor("table0", [2 * ROWS + P, W0], f32).ap()
    table1 = nc.dram_tensor("table1", [2 * ROWS + P, D], f32).ap()
    x1_dram = nc.dram_tensor("x1_dram", [ROWS, D], f32).ap()

    def rows4(t, g):
        return t[bass.ds(g * (T * P), T * P), :].rearrange("(j p) f -> p j f", p=P)

    ctx = ExitStack()
    with ctx:
        def sb(name, shape, dt=f32):
            return ctx.enter_context(nc.sbuf_tensor(name, shape, dt))

        def sem(name):
            return ctx.enter_context(nc.semaphore(name))

        ring_at = sb("ring_at", [1, TILES], i32)
        wide = sb("wide", [1, GROUPS], i32)
        wide_f = sb("wide_f", [1, GROUPS])
        offs_i = sb("offs_i", [1, TILES], i32)
        flag_i = sb("flag_i", [1, 4], i32)
        ident = sb("ident", [P, P])
        iota = sb("iota", [P, TILES + 4])
        tile_base = sb("tile_base", [P, TILES + 4])
        tile_no = sb("tile_no", [TILES // 4, SPAN, 4])
        started = sb("started", [TILES // 4, 4, TILES + 1], bf16)
        dst_rows = sb("dst_rows", [TILES // 4, 2, 4, P], bf16)
        offs = sb("offs", [1, TILES])
        rel = sb("rel", [P, GROUPS, SPAN, T])
        count4 = sb("count4", [P, LOW, T], f16)
        src_i = sb("src_i", [P, TILES], i32)
        dst_i = sb("dst_i", [P, TILES], i32)
        src_use = sb("src_use", [P, TILES], i32)
        dst_f = sb("dst_f", [P, TILES])
        part_i = sb("part_i", [P, TILES], i32)
        digits = sb("digits", [P, 4, TILES], f16)
        c_send = sb("c_send", [P, TILES])
        rn = sb("rn", [P, TILES])
        rinv = sb("rinv", [P, TILES])
        norm1 = sb("norm1", [P, TILES])
        rstd1 = sb("rstd1", [P, TILES])
        nb1 = sb("nb1", [P, TILES])
        deg = sb("deg", [P, 3, TILES])
        dsq = sb("dsq", [P, 3, TILES])
        before = sb("before", [P, P + 1])
        z_edge = sb("z_edge", [P, P])
        z_rows = sb("z_rows", [P, W0])
        z_pre = sb("z_pre", [P, D])
        z_msg = sb("z_msg", [P, W0])
        z_node = sb("z_node", [P, P])
        z_same = sb("z_same", [P, P])
        z_dup = sb("z_dup", [P, P])
        z_cnt = sb("z_cnt", [P, 4])
        z_src = sb("z_src", [P, 1], i32)
        z_dst = sb("z_dst", [P, 1], i32)
        z_sum = sb("z_sum", [P, W0])
        z_scr = sb("z_scr", [P, 4], i32)
        first_i = sb("first_i", [TILES // 4, 4], i32)
        first_f = sb("first_f", [TILES // 4, 4])
        a_f = sb("a_f", [P, TILES + 1])
        bad = sb("bad", [P, 8])
        group_tile = sb("group_tile", [P, TILES])
        badrow = sb("badrow", [P, 2, TILES])
        ones = sb("ones", [P, P])
        ones_b = sb("ones_b", [P, P], bf16)
        ones3 = sb("ones3", [3, P], bf16)
        eps_t = sb("eps_t", [P, 1])
        b_rows = sb("b_rows", [P, D])
        wn = sb("wn", [P, D])
        we = sb("we", [P, D])
        w1 = sb("w1", [P, 2, D])
        brow = sb("brow", [3, 3, D])
        bsum = sb("bsum", [3, 2, D])
        bres = sb("bres", [3, 2, D])
        idx = sb("idx", [P, 4, T], i32)
        bpart = sb("bpart", [3, 3, 2, D], bf16)
        bsel = sb("bsel", [3, 2, D])
        bias4 = sb("bias4", [3, 2, T, D], bf16)
        low_hot = sb("low_hot", [P, 2, LOW, T], bf16)
        high_hot = sb("high_hot", [P, 2, HIGH, T], bf16)

        xb = sb("xb", [P, 8, T, D])
        ya = sb("ya", [P, 4, T, W0])
        h = sb("h", [P, 4, T, D])
        agg = sb("agg", [P, 2, T, D])
        hT = sb("hT", [P, 2, T * P])
        aT = sb("aT", [P, 2, T * P])
        gath = sb("gath", [P, 8, T, W0])
        edge = sb("edge", [P, 4, T * P])
        ring = sb("ring", [P, RING + SPAN - 1, D])
        ring_flat = ring[:, :, :].rearrange("p r f -> p (r f)")
        chosen = ring_flat[0:TILES // 4, 0:SPAN * 4 * TILES // 2].bitcast(bf16).rearrange(
            "p (w c t) -> p w c t", w=SPAN, c=4)
        pick = sb("pick", [P, 2, T * SPAN, P])
        early = pick[:, :, :, :].rearrange("p b k m -> p (b k m)")
        early_i = early.bitcast(i32)
        cur_i, next_i = early_i[:, 0:TILES], early_i[:, TILES:2 * TILES]
        cur_f, next_f = early[:, 2 * TILES:3 * TILES], early[:, 3 * TILES:4 * TILES]
        dst_rows_i = early_i[0:TILES // 4, 4 * TILES:4 * TILES + 4 * P].rearrange("p (c e) -> p c e", c=4)
        dst_part = early_i[0:TILES // 4, 5 * TILES + P:5 * TILES + 5 * P].rearrange("p (c e) -> p c e", c=4)
        q = sb("q", [P, 2, T, D])
        v = sb("v", [P, T, D])
        x1 = sb("x1", [P, 4, T, D])
        bnst = sb("bnst", [P, 2, T, 6])
        mv = sb("mv", [P, 4, T, 2])
        sd = sb("sd", [P, 4, T])
        rs = sb("rs", [P, 4, T])
        nb = sb("nb", [P, 4, T])
        sc1 = sb("sc1", [P, 4, T])
        bi1 = sb("bi1", [P, 4, T])
        junk = sb("junk", [P, T, D])
        ss = sb("ss", [P, 4, T])
        nrm = sb("nrm", [P, 4, T])
        inv = sb("inv", [P, 4, T])

        bank = [ctx.enter_context(nc.psum_tensor(f"bank{i}", [P, 512], f32)) for i in range(8)]

        names = """consts_in idx_in order_in started_rdy chosen_rdy rel_psum rel_used bias_rdy setup ones_rdy a_psum bad_psum flag_rdy tables_rdy deg_sum deg_sqrt
            hot_rdy hist_done x_in0 x_in1 x_in2 x_in3 n_bn n_stats n_sd n_rs n_coef n_h n_tp n_hT n_mm
            n_evac n_col t0_out0 t0_out1 t0_out2 t0_out3 idx_rdy
            g_in0 g_in1 g_in2 g_in3 e_in0 e_in1 e_in2 e_in3 y_in0 y_in1 y_in2 y_in3 xl_in0 xl_in1 xl_in2
            xl_in3 emm_done sum_rdy msg_rdy pick_rdy seg_done q_rdy v_rdy x1_rdy l_bn l_stats l_sd l_rs
            l_nb l_coef t1_rdy x1_out0 x1_out1 x1_out2 x1_out3 t1_out0 t1_out1 t1_out2 t1_out3
            r_in0 r_in1 r_in2 r_in3 xx_in0 xx_in1 xx_in2 xx_in3 o_again o_pick o_seg o_agg o_h o_h2 o_tp o_hT o_aT
            o_mm o_sum o_sq o_nrm o_inv o_y y_out0 y_out1 y_out2 y_out3
            z0_zero z0_init z0_edge z0_idx z0_src z0_emm z0_tgt z0_msg z0_same z0_sum z0_scat z0_mvin z0_mvout z0_carry z0_reset
            z1_zero z1_init z1_edge z1_idx z1_src z1_emm z1_tgt z1_msg z1_same z1_sum z1_scat z1_mvin z1_mvout z1_carry z_chain""".split()
        S = {n: sem(n) for n in names}

        def need(eng, s, value):
            if isinstance(value, int) and value <= 0:
                return
            eng.wait_ge(s, value)

        def rounds(eng, step, lag):
            full = GROUPS // U
            for i in range(PEEL):
                for u in range(U):
                    step(i, u)
            with eng.Fori(PEEL, full) as i:
                for u in range(U):
                    step(i, u)
            for s in range(full * U, GROUPS + lag):
                step(s // U, s % U)

        def grp(i, u, lag):
            g = i * U + (u - lag)
            if isinstance(g, int) and not 0 <= g < GROUPS:
                return None
            return g, (u - lag) % 4, i * (U // 4) + (u - lag) // 4

        def eighth(u, lag):
            return (u - lag) % 8

        def ring_places_of(u, lag, j):
            place = eighth(u, lag) * T + j
            return (place, RING + place) if place < SPAN - 1 else (place,)

        def edge_bank(slot):
            return bank[(0, 1, 4, 5)[slot]]

        LAPS = [len(range(k, GROUPS, 4)) for k in range(4)]

        block = ctx.enter_context(nc.Block())

        def flag_of(eng):
            eng.wait_ge(S["flag_rdy"], 1)
            return eng.value_load(flag_i[0:1, 0:1], min_val=0, max_val=1 << 10)

        def ring_places(after):
            V = nc.vector
            after(V.tensor_scalar(offs[:, :], a_f[0:1, 0:TILES], float(D), None, ALU.mult))
            after(V.tensor_copy(offs_i[:, :], offs[:, :]))
            after(V.tensor_single_scalar(ring_at[:, :], offs_i[:, :], (RING - 1) * D, ALU.bitwise_and))

        def general_loads(sp, layer):
            table = (table0, table1)[layer]
            w = (W0, D)[layer]
            z = {n: S[f"z{layer}_{n}"] for n in ("zero", "init", "edge", "scat", "mvin", "mvout")}
            zeros, low, high = gath[:, 0, :, 0:w], gath[:, 1, :, 0:w], gath[:, 2, :, 0:w]
            sp.wait_ge(z["zero"], 1)
            sp.dma_start(table[2 * ROWS:, :], gath[:, 0, 0, 0:w]).then_inc(z["init"], 16)
            with sp.Fori(GROUPS, 2 * GROUPS) as g:
                sp.dma_start(rows4(table, g), zeros).then_inc(z["init"], 16)
            if layer == 0:
                sp.dma_start(z_edge[:, :], edgeT[:, 0:P]).then_inc(z["edge"], 16)
                with sp.Fori(1, TILES) as k:
                    sp.wait_ge(z["scat"], k * 16)
                    sp.dma_start(z_edge[:, :], edgeT[:, bass.ds(k * P, P)]).then_inc(z["edge"], 16)
            sp.wait_ge(z["scat"], 16 * TILES)

            def move(g):
                sp.dma_start(low, rows4(table, g)).then_inc(z["mvin"], 16)
                sp.dma_start(high, rows4(table, g + GROUPS)).then_inc(z["mvin"], 16)
                sp.wait_ge(z["mvin"], g * 32 + 32)
                sp.dma_start(rows4(table, g), high).then_inc(z["mvout"], 16)
                sp.dma_start(rows4(table, g + GROUPS), low).then_inc(z["mvout"], 16)

            move(0)
            with sp.Fori(1, GROUPS) as g:
                sp.wait_ge(z["mvout"], g * 32)
                move(g)
            sp.wait_ge(z["mvout"], 32 * GROUPS)

        def own_rows(sp, bad_n, n):
            first = n * (T * P) + (bad_n > 0) * ROWS
            return table0[bass.ds(first, T * P), :].rearrange("(j p) f -> p j f", p=P)

        def general_gathers(pool, layer):
            table = (table0, table1)[layer]
            w = (W0, D)[layer]
            z = {n: S[f"z{layer}_{n}"] for n in ("init", "idx", "src", "sum", "scat", "mvout", "carry")}
            pool.wait_ge(z["init"], 16 * (GROUPS + 1))

            def tile(k):
                pool.wait_ge(z["idx"], k + 1)
                nc.gpsimd.tensor_tensor(z_scr[:, 0:1], z_scr[:, 2:3], z_scr[:, 3:4], ALU.add).then_inc(
                    z["carry"], 1)
                pool.indirect_dma_start(
                    out=z_rows[:, 0:w], out_offset=None, in_=table[0:ROWS, :],
                    in_offset=bass.IndirectOffsetOnAxis(ap=z_src[:, :], axis=0),
                    bounds_check=ROWS - 1, oob_is_err=False).then_inc(z["src"], 16)
                pool.wait_ge(z["sum"], k + 1)
                nc.gpsimd.tensor_tensor(z_scr[:, 1:2], z_scr[:, 2:3], z_scr[:, 3:4], ALU.add).then_inc(
                    z["carry"], 1)
                pool.indirect_dma_start(
                    in_=z_sum[:, 0:w], in_offset=None, out=table[:, :],
                    out_offset=bass.IndirectOffsetOnAxis(ap=z_dst[:, :], axis=0),
                    bounds_check=2 * ROWS + P - 1, oob_is_err=True,
                    compute_op=ALU.add).then_inc(z["scat"], 16)

            with pool.Fori(0, TILES) as k:
                tile(k)
            pool.wait_ge(z["mvout"], 32 * GROUPS)
            if layer == 0:
                pool.wait_ge(S["z0_reset"], 1)

        def general_vector(dve, layer):
            V = nc.vector
            w = (W0, D)[layer]
            z = {n: S[f"z{layer}_{n}"] for n in ("zero", "idx", "src", "emm", "tgt", "same", "sum", "scat", "carry")}
            V.memset(gath[:, 0, :, 0:D], 0.0)
            V.memset(gath[:, 0, :, D:], 1.0)
            V.memset(z_scr[:, :], 0)
            V.memset(z_msg[:, D:], 0.0).then_inc(z["zero"], 1)

            def tile(k, first=False):
                if not first:
                    dve.wait_ge(z["scat"], k * 16)
                    dve.wait_ge(z["carry"], k * 2)
                V.tensor_copy(z_src[:, :], src_i[:, bass.ds(k, 1)])
                V.tensor_copy(z_node[:, :], dst_f[:, bass.ds(k, 1)].to_broadcast([P, P])).then_inc(z["idx"], 1)
                dve.wait_ge(z["emm"], k + 1)
                V.tensor_scalar(z_same[:, :], bank[5][:, 0:P], dst_f[:, bass.ds(k, 1)], None,
                                ALU.is_equal).then_inc(z["tgt"], 1)
                dve.wait_ge(z["src"], k * 16 + 16)
                if layer == 0:
                    V.tensor_tensor(z_pre[:, :], bank[7][:, 0:D], z_rows[:, 0:D], ALU.add)
                else:
                    V.tensor_copy(z_msg[:, 0:D], z_rows[:, 0:D])
                dve.wait_ge(z["tgt"], k * 5 + 1)
                V.tensor_tensor(z_dup[:, :], z_same[:, :], before[:, 0:P], ALU.mult).then_inc(z["tgt"], 1)
                dve.wait_ge(z["tgt"], k * 5 + 2)
                V.reduce_sum(z_cnt[:, 0:1], z_dup[:, :], AX)
                V.tensor_scalar(z_cnt[:, 1:2], dst_f[:, bass.ds(k, 1)], before[:, P:], -float(ROWS),
                                ALU.subtract, ALU.add).then_inc(z["tgt"], 1)
                dve.wait_ge(z["tgt"], k * 5 + 3)
                V.scalar_tensor_tensor(z_cnt[:, 2:3], z_cnt[:, 0:1], 0.0, z_cnt[:, 1:2],
                                       ALU.is_equal, ALU.mult).then_inc(z["tgt"], 1)
                dve.wait_ge(z["tgt"], k * 5 + 4)
                V.tensor_scalar(z_dst[:, :], z_cnt[:, 2:3], before[:, P:], 2.0 * ROWS, ALU.add,
                                ALU.add).then_inc(z["tgt"], 1)
                dve.wait_ge(z["same"], k + 1)
                dve.wait_ge(z["tgt"], k * 5 + 5)
                V.tensor_copy(z_sum[:, 0:w], bank[6][:, 0:w]).then_inc(z["sum"], 1)

            tile(0, True)
            with dve.Fori(1, TILES) as k:
                tile(k)
            dve.wait_ge(z["scat"], 16 * TILES)
            if layer == 0:
                count = [0]

                def after(ins):
                    count[0] += 1
                    ins.then_inc(S["z_chain"], 1)
                    dve.wait_ge(S["z_chain"], count[0])

                after(V.tensor_scalar(src_use[:, :], tile_base[:, 0:TILES], before[:, P:], None, ALU.add))
                after(V.tensor_scalar(a_f[:, 0:TILES], iota[:, 0:TILES], -1.0, 0.0, ALU.add, ALU.max))
                ring_places(after)
                V.memset(wide[:, :], 0)
                after(V.tensor_tensor(badrow[:, 0, :], a_f[:, 0:TILES], iota[:, 0:TILES], ALU.subtract))
                after(V.tensor_scalar(badrow[:, 1, :], badrow[:, 0, :], float(P), None, ALU.mult))
                after(V.tensor_scalar(badrow[:, 0, :], badrow[:, 1, :], before[:, P:], None, ALU.add))
                for k in range(SPAN):
                    after(V.tensor_scalar(rel[:, :, k, :], badrow[:, 0, :].rearrange("p (g j) -> p g j", j=T),
                                          float(P * k), None, ALU.add))
                V.memset(we[:, :], 0.0)
                V.memset(bias4[:, 1, :, :], 0.0).then_inc(S["z0_reset"], 1)
                dve.wait_ge(S["z0_reset"], 1)

        def general_products(pe, layer):
            w = (W0, D)[layer]
            z = {n: S[f"z{layer}_{n}"] for n in ("idx", "edge", "emm", "tgt", "msg", "same")}

            def tile(k):
                pe.wait_ge(z["idx"], k + 1)
                if layer == 0:
                    pe.wait_ge(z["edge"], k * 16 + 16)
                    nc.tensor.matmul(bank[7][:, 0:D], ones3[:, :], bias4[:, 1, 0, :], start=True, stop=False)
                    nc.tensor.matmul(bank[7][:, 0:D], z_edge[:, :], we[:, :], start=False, stop=True)
                nc.tensor.transpose(bank[5][:, 0:P], z_node[:, :], ident[:, :]).then_inc(z["emm"], 1)
                if layer == 0:
                    pe.wait_ge(z["msg"], k + 1)
                pe.wait_ge(z["tgt"], k * 5 + 2)
                nc.tensor.matmul(bank[6][:, 0:w], z_same[:, :], z_msg[:, 0:w], start=True,
                                 stop=True).then_inc(z["same"], 1)

            with pe.Fori(0, TILES) as k:
                tile(k)
            if layer == 0:
                pe.wait_ge(S["z0_reset"], 1)

        def general_messages(act):
            z = {n: S[f"z0_{n}"] for n in ("tgt", "msg")}
            with act.Fori(0, TILES) as k:
                act.wait_ge(z["tgt"], k * 5 + 2)
                nc.scalar.activation(z_msg[:, 0:D], z_pre[:, :], ACT.Relu,
                                     scale=z_rows[:, D:]).then_inc(z["msg"], 1)

        @block.sync
        def _(sp):
            for dst, src in ((src_i, srcT), (iota, iota_in), (first_i, dst_first), (tile_base, tile_base_in)):
                sp.dma_start(dst[:, :], src).then_inc(S["idx_in"], 16)
            for dst, src in ((dst_i, dstT), (ident, ident_in), (wn, w_node), (we, w_edge),
                             (b_rows, b_out)):
                sp.dma_start(dst[:, :], src).then_inc(S["consts_in"], 16)
            sp.dma_start(w1[:, :, :], w_out.rearrange("(k p) f -> p k f", p=P)).then_inc(S["consts_in"], 16)
            for r in range(3):
                for k, b in enumerate((b_node, b_edge, root)):
                    sp.dma_start(brow[r:r + 1, k, :], b).then_inc(S["consts_in"], 16)
            for dst, src in ((before, before_in), (group_tile, group_tile_in), (cur_i, dst_cur),
                             (next_i, dst_next)):
                sp.dma_start(dst[:, :], src).then_inc(S["order_in"], 16)
            sp.dma_start(tile_no[:, :, :], tile_no_in).then_inc(S["order_in"], 16)
            sp.dma_start(dst_rows_i[:, :, :], dst_rows_in).then_inc(S["order_in"], 16)

            def load_nodes(i, u):
                g = grp(i, u, 0)
                if g:
                    g, slot, r = g
                    need(sp, S["n_h"], g - 7)
                    need(sp, S[f"x_in{slot}"], 16 * r)
                    sp.dma_start(xb[:, eighth(u, 0), :, :], rows4(x, g)).then_inc(S[f"x_in{slot}"], 16)

            rounds(sp, load_nodes, 0)

            for k in range(4):
                sp.wait_ge(S[f"t0_out{k}"], 16 * LAPS[k])

            bad_n = flag_of(sp)
            with sp.If(bad_n > 0):
                general_loads(sp, 0)

            def load_layer0(i, u):
                g = grp(i, u, 0)
                if g:
                    g, slot, r = g
                    need(sp, S["emm_done"], g - 3)
                    sp.dma_start(edge[:, slot, :], edgeT[:, bass.ds(g * (T * P), T * P)]).then_inc(
                        S[f"e_in{slot}"], 16)
                n = grp(i, u, 3)
                if n:
                    n, slot, r = n
                    need(sp, S["q_rdy"], n - 3)
                    sp.dma_start(ya[:, slot, :, :], own_rows(sp, bad_n, n)).then_inc(S[f"y_in{slot}"], 16)
                n = grp(i, u, 4)
                if n:
                    n, slot, r = n
                    need(sp, S["x1_rdy"], n - 3)
                    sp.dma_start(xb[:, slot, :, :], rows4(x, n)).then_inc(S[f"xl_in{slot}"], 16)

            sp.wait_ge(S["n_h"], GROUPS)
            rounds(sp, load_layer0, 4)

            for k in range(4):
                sp.wait_ge(S[f"x1_out{k}"], 16 * LAPS[k])
                sp.wait_ge(S[f"t1_out{k}"], 16 * LAPS[k])

            with sp.If(bad_n > 0):
                general_loads(sp, 1)

            def load_layer1(i, u):
                g = grp(i, u, 0)
                if g:
                    g, slot, r = g
                    need(sp, S["o_y"], g - 7)
                    need(sp, S[f"xx_in{slot}"], 16 * r)
                    sp.dma_start(xb[:, eighth(u, 0), :, :], rows4(x1_dram, g)).then_inc(S[f"xx_in{slot}"], 16)

            sp.wait_ge(S["x1_rdy"], GROUPS)
            rounds(sp, load_layer1, 0)

        @block.gpsimd
        def _(pool):
            def gather(dst, table, col, landed):
                pool.indirect_dma_start(
                    out=dst, out_offset=None, in_=table,
                    in_offset=bass.IndirectOffsetOnAxis(ap=col, axis=0),
                    bounds_check=ROWS - 1, oob_is_err=False).then_inc(landed, 16)

            for k in range(4):
                pool.wait_ge(S[f"t0_out{k}"], 16 * LAPS[k])

            bad_n = flag_of(pool)
            with pool.If(bad_n > 0):
                general_gathers(pool, 0)

            def place_indices(g, slot):
                nc.gpsimd.tensor_copy(idx[:, slot, :], src_use[:, bass.ds(g * T, T)]).then_inc(
                    S["idx_rdy"], 1)

            def fetch0(i, u):
                g = grp(i, u, 0)
                if g:
                    g, slot, r = g
                    pool.wait_ge(S["idx_rdy"], g + 1)
                    need(pool, S["msg_rdy"], g - 7)
                    n = grp(i, u, -1)
                    if n:
                        need(pool, S[f"g_in{n[1]}"], 64 * n[2])
                        place_indices(*n[:2])
                    for j in range(T):
                        gather(gath[:, eighth(u, 0), j, :], table0[0:ROWS, :], idx[:, slot, j:j + 1], S[f"g_in{slot}"])

            place_indices(0, 0)
            rounds(pool, fetch0, 0)

            for k in range(4):
                pool.wait_ge(S[f"t1_out{k}"], 16 * LAPS[k])
                pool.wait_ge(S[f"g_in{k}"], 64 * LAPS[k])
            pool.wait_ge(S["seg_done"], GROUPS)

            with pool.If(bad_n > 0):
                general_gathers(pool, 1)

            def fetch1(i, u):
                g = grp(i, u, 0)
                if g:
                    g, slot, r = g
                    pool.wait_ge(S["idx_rdy"], GROUPS + g + 1)
                    need(pool, S["o_seg"], g - 5)
                    n = grp(i, u, -1)
                    if n:
                        need(pool, S[f"r_in{n[1]}"], 64 * n[2])
                        place_indices(*n[:2])
                    for j in range(T):
                        gather(ring[:, eighth(u, 0) * T + j, :], table1[0:ROWS, :], idx[:, slot, j:j + 1],
                               S[f"r_in{slot}"])

            place_indices(0, 0)
            rounds(pool, fetch1, 0)

        @block.vector
        def _(dve):
            chain = [0]

            def link(ins):
                chain[0] += 1
                ins.then_inc(S["setup"], 1)
                dve.wait_ge(S["setup"], chain[0])

            V = nc.vector
            link(V.memset(ones3[:, :], 1.0))
            link(V.memset(eps_t[:, :], EPS))
            link(V.memset(ones[:, :], 1.0))
            V.memset(ones_b[:, :], 1.0).then_inc(S["ones_rdy"], 1)

            def split_ids(k, ids):
                for part, amount, op in ((2 * k, LOW - 1, ALU.bitwise_and),
                                         (2 * k + 1, 8, ALU.logical_shift_right)):
                    link(V.tensor_single_scalar(part_i[:, :], ids[:, :], amount, op))
                    link(V.tensor_copy(digits[:, part, :], part_i[:, :]))

            dve.wait_ge(S["idx_in"], 16 * 4)
            link(V.tensor_copy(first_f[:, :], first_i[:, :]))
            for c in range(4):
                ins = V.tensor_scalar(started[:, c, :], tile_base[0:TILES // 4, 0:TILES + 1],
                                      first_f[:, c:c + 1], None, ALU.is_gt)
            ins.then_inc(S["started_rdy"], 1)
            link(V.tensor_copy(count4[:, :, :], iota[:, 0:LOW].unsqueeze(2).to_broadcast([P, LOW, T])))
            split_ids(0, src_i)

            def one_hots(n, k):
                g, slot, r = n
                need(dve, S["hist_done"], g + (k * GROUPS - 1))
                at = bass.ds(g * T, T)
                for hot, part, size in ((low_hot, 2 * k, LOW), (high_hot, 2 * k + 1, HIGH)):
                    ins = V.tensor_tensor(hot[:, slot % 2, :, :], count4[:, 0:size, :],
                                          digits[:, part, at].unsqueeze(1).to_broadcast([P, size, T]),
                                          ALU.is_equal)
                ins.then_inc(S["hot_rdy"], 1)

            def degrees(k, which, extra, op):
                return V.tensor_scalar(deg[:, which, :].rearrange("p (h b) -> p b h", b=LOW // P),
                                       bank[2 + k][:, 0:TILES].rearrange("p (b h) -> p b h", b=LOW // P),
                                       extra, None, op)

            def send_step(i, u):
                g = grp(i, u, 0)
                if g:
                    one_hots(g, 0)

            rounds(dve, send_step, 0)
            dve.wait_ge(S["consts_in"], 16 * 15)
            split_ids(1, dst_i)
            link(V.tensor_tensor(bsum[:, 0, :], brow[:, 0, :], brow[:, 2, :], ALU.add))
            link(V.tensor_tensor(bsum[:, 1, :], brow[:, 1, :], brow[:, 2, :], ALU.subtract))
            link(V.tensor_copy(bpart[:, 0, :, :], bsum[:, :, :]))
            link(V.tensor_tensor(bres[:, :, :], bsum[:, :, :], bpart[:, 0, :, :], ALU.subtract))
            link(V.tensor_copy(bpart[:, 1, :, :], bres[:, :, :]))
            link(V.tensor_tensor(bres[:, :, :], bres[:, :, :], bpart[:, 1, :, :], ALU.subtract))
            link(V.tensor_copy(bpart[:, 2, :, :], bres[:, :, :]))
            link(V.tensor_scalar(bsel[:, :, :], bpart[:, 0, :, :], ident[0:3, 0:1], None, ALU.mult))
            link(V.scalar_tensor_tensor(bsel[:, :, :], bpart[:, 1, :, :], ident[0:3, 1:2], bsel[:, :, :],
                                        ALU.mult, ALU.add))
            link(V.scalar_tensor_tensor(bsel[:, :, :], bpart[:, 2, :, :], ident[0:3, 2:3], bsel[:, :, :],
                                        ALU.mult, ALU.add))
            for j in range(T):
                ins = V.tensor_copy(bias4[:, :, j, :], bsel[:, :, :])
            ins.then_inc(S["bias_rdy"], 1)
            dve.wait_ge(S["hist_done"], GROUPS)
            degrees(0, 0, 1.0, ALU.add).then_inc(S["deg_sum"], 1)
            dve.wait_ge(S["deg_sqrt"], 1)
            V.reciprocal(c_send[:, :], dsq[:, 0, :]).then_inc(S["tables_rdy"], 1)
            dve.wait_ge(S["tables_rdy"], 1)

            def node_step(i, u):
                now = grp(i, u, 0)
                if now:
                    g, slot, r = now
                    dve.wait_ge(S[f"x_in{slot}"], 16 * (r + 1))
                    for j in range(T):
                        ins = V.bn_stats(bnst[:, slot % 2, j, :], xb[:, eighth(u, 0), j, :])
                    ins.then_inc(S["n_bn"], 1)
                last = grp(i, u, 1)
                if last:
                    m, mslot, mr = last
                    dve.wait_ge(S["n_sd"], m + 1)
                    V.reciprocal(rs[:, mslot, :], sd[:, mslot, :]).then_inc(S["n_rs"], 1)
                if now:
                    dve.wait_ge(S["n_bn"], g + 1)
                    need(dve, S["n_h"], g - 3)
                    one_hots(now, 1)
                if last:
                    dve.wait_ge(S["n_rs"], m + 1)
                    V.scalar_tensor_tensor(nb[:, mslot, :], mv[:, mslot, :, 0], -1.0, rs[:, mslot, :],
                                           ALU.mult, ALU.mult).then_inc(S["n_coef"], 1)
                c = grp(i, u, 5)
                if c:
                    need(dve, S[f"t0_out{c[1]}"], 16 * c[2])
                    V.tensor_copy(ya[:, c[1], :, D], c_send[:, bass.ds(c[0] * T, T)]).then_inc(S["n_col"], 1)
                if now:
                    for j in range(T):
                        ins = V.bn_aggr(mv[:, slot, j, :], bnst[:, slot % 2, j, :])
                    ins.then_inc(S["n_stats"], 1)

            rounds(dve, node_step, 5)
            dve.wait_ge(S["order_in"], 16 * 6)
            link(V.tensor_copy(dst_f[:, :], dst_i[:, :]))
            dve.wait_ge(S["a_psum"], 1)
            link(V.tensor_scalar(a_f[:, :], bank[0][:, 0:TILES + 1], -1.0, 0.0, ALU.add, ALU.max))
            V.tensor_copy(src_use[:, :], src_i[:, :])
            V.tensor_copy(cur_f[:, :], cur_i[:, :])
            link(V.tensor_copy(next_f[:, :], next_i[:, :]))
            link(V.tensor_tensor(badrow[:, 0, :], cur_f[:, :], next_f[:, :], ALU.is_gt))
            link(V.reduce_max(bad[:, 0:1], badrow[:, 0, :], AX))
            link(V.tensor_tensor(badrow[:, 0, :], a_f[:, 1:TILES + 1], a_f[:, 0:TILES], ALU.subtract))
            link(V.reduce_max(wide_f[:, :], badrow[0:1, 0, :].rearrange("p (g j) -> p g j", j=T), AX))
            link(V.tensor_scalar(wide[:, :], wide_f[:, :], SPAN - 2.0, None, ALU.is_gt))
            link(V.tensor_scalar(badrow[:, 0, :], badrow[:, 0, :], SPAN - 1.0, None, ALU.is_gt))
            link(V.reduce_max(bad[:, 1:2], badrow[:, 0, :], AX))
            link(V.tensor_tensor(badrow[:, 0, :], a_f[:, 0:TILES], group_tile[:, :], ALU.subtract))
            link(V.tensor_scalar(badrow[:, 1, :], badrow[:, 0, :], -float(BACK), None, ALU.is_lt))
            link(V.reduce_max(bad[:, 2:3], badrow[:, 1, :], AX))
            link(V.tensor_scalar(badrow[:, 1, :], badrow[:, 0, :], float(AHEAD), None, ALU.is_gt))
            link(V.reduce_max(bad[:, 3:4], badrow[:, 1, :], AX))
            V.reduce_sum(bad[:, 4:5], bad[:, 0:4], AX).then_inc(S["bad_psum"], 1)

            for k in range(SPAN):
                for c in range(4):
                    V.tensor_scalar(chosen[:, k, c, :], a_f[0:TILES // 4, 0:TILES], tile_no[:, k, c:c + 1],
                                    None, ALU.is_equal)
            for part, mask in enumerate((LOW - 1, ((1 << 16) - 1) & ~(LOW - 1))):
                link(V.tensor_single_scalar(dst_part[:, :, :], dst_rows_i[:, :, :], mask, ALU.bitwise_and))
                ins = V.tensor_copy(dst_rows[:, part, :, :], dst_part[:, :, :])
                if part == 0:
                    link(ins)
            ins.then_inc(S["chosen_rdy"], 1)
            dve.wait_ge(S["bad_psum"], 2)
            V.tensor_copy(flag_i[0:1, 0:1], bank[1][0:1, 0:1]).then_inc(S["flag_rdy"], 1)
            ring_places(link)
            dve.wait_ge(S["hist_done"], 2 * GROUPS)
            degrees(1, 1, 1.0, ALU.add)
            degrees(1, 2, 1.0, ALU.max).then_inc(S["deg_sum"], 1)
            dve.wait_ge(S["deg_sum"], 2)
            V.reciprocal(rinv[:, :], deg[:, 1, :])
            dve.wait_ge(S["deg_sqrt"], 2)
            V.reciprocal(rn[:, :], dsq[:, 1, :])
            V.reciprocal(norm1[:, :], dsq[:, 2, :]).then_inc(S["tables_rdy"], 1)
            dve.wait_ge(S["tables_rdy"], 2)
            dve.wait_ge(S["rel_psum"], 1)
            for k in range(SPAN):
                ins = V.tensor_tensor(rel[:, :, k, :], bank[5 + k][:, 0:TILES].rearrange("p (g j) -> p g j", j=T),
                                      tile_base[:, 0:TILES].rearrange("p (g j) -> p g j", j=T), ALU.subtract)
            ins.then_inc(S["rel_used"], 1)
            dve.wait_ge(S["rel_used"], 1)

            def third_of(n):
                return dve.value_load(wide[0:1, bass.ds(n, 1)], min_val=0, max_val=1)

            rel_flat = rel[:, :, :, :].rearrange("p g w j -> p (g w j)")

            def picks(n, third, par, ready):
                def some(first, size):
                    return V.tensor_tensor(
                        pick[:, par, first:first + size, :],
                        iota[:, 0:P].unsqueeze(1).to_broadcast([P, size, P]),
                        rel_flat[:, bass.ds(n * (SPAN * T) + first, size)].unsqueeze(2).to_broadcast([P, size, P]),
                        ALU.is_equal)

                some(0, T)
                with dve.If(third > 0):
                    some(2 * T, T)
                some(T, T).then_inc(ready, 1)

            for k in range(4):
                dve.wait_ge(S[f"t0_out{k}"], 16 * LAPS[k])
            bad_n = flag_of(dve)
            with dve.If(bad_n > 0):
                general_vector(dve, 0)

            def layer0_step(i, u):
                last = grp(i, u, LAG + 2)
                if last:
                    m, mslot, mr = last
                    dve.wait_ge(S["l_bn"], m + 1)
                now = grp(i, u, LAG + 1)
                if now:
                    n, slot, r = now
                    dve.wait_ge(S["seg_done"], n + 1)
                    dve.wait_ge(S["q_rdy"], n + 1)
                    for j in range(T):
                        ins = V.scalar_tensor_tensor(v[:, j, :], bank[2 + slot % 2][:, j * D:(j + 1) * D],
                                                     rn[:, bass.ds(n * T + j, 1)], q[:, slot % 2, j, :],
                                                     ALU.mult, ALU.add)
                    ins.then_inc(S["v_rdy"], 1)
                if last:
                    for j in range(T):
                        ins = V.bn_aggr(mv[:, mslot, j, :], bnst[:, mslot % 2, j, :])
                    ins.then_inc(S["l_stats"], 1)
                if now:
                    dve.wait_ge(S["v_rdy"], n + 1)
                    dve.wait_ge(S[f"xl_in{slot}"], 16 * (r + 1))
                    need(dve, S[f"x1_out{slot}"], 16 * r)
                    V.scalar_tensor_tensor(x1[:, slot, :, :], v[:, :, :], 0.0, xb[:, slot, :, :],
                                           ALU.max, ALU.add).then_inc(S["x1_rdy"], 1)
                p = grp(i, u, LAG - 1)
                if p:
                    third = third_of(p[0])
                    need(dve, S["seg_done"], p[0] - 1)
                    picks(p[0], third, p[1] % 2, S["pick_rdy"])
                if last:
                    at = bass.ds(m * T, T)
                    dve.wait_ge(S["l_sd"], m + 1)
                    V.reciprocal(rstd1[:, at], sd[:, mslot, :]).then_inc(S["l_rs"], 1)
                if now:
                    dve.wait_ge(S["x1_rdy"], n + 1)
                    for j in range(T):
                        ins = V.bn_stats(bnst[:, slot % 2, j, :], x1[:, slot, j, :])
                    ins.then_inc(S["l_bn"], 1)
                if last:
                    dve.wait_ge(S["l_rs"], m + 1)
                    V.scalar_tensor_tensor(nb1[:, at], mv[:, mslot, :, 0], -1.0, rstd1[:, at],
                                           ALU.mult, ALU.mult).then_inc(S["l_nb"], 1)
                    V.tensor_tensor(sc1[:, mslot, :], rstd1[:, at], norm1[:, at], ALU.mult)
                    dve.wait_ge(S["l_nb"], m + 1)
                    V.tensor_tensor(bi1[:, mslot, :], nb1[:, at], norm1[:, at], ALU.mult).then_inc(
                        S["l_coef"], 1)

            rounds(dve, layer0_step, LAG + 2)

            def layer1_step(i, u):
                n = grp(i, u, 6)
                if n:
                    n, slot, r = n
                    dve.wait_ge(S["o_mm"], n + 1)
                    need(dve, S[f"y_out{slot}"], 16 * r)
                    V.tensor_tensor(x1[:, slot, :, :],
                                    bank[2 + slot % 2][:, :].rearrange("p (j f) -> p j f", f=D),
                                    b_rows[:, :].unsqueeze(1).to_broadcast([P, T, D]),
                                    ALU.add).then_inc(S["o_sum"], 1)
                n = grp(i, u, 0)
                if n:
                    n, slot, r = n
                    third = third_of(n)
                    need(dve, S["o_seg"], n - 1)
                    picks(n, third, slot % 2, S["o_pick"])
                n = grp(i, u, 2)
                if n:
                    n, slot, r = n
                    dve.wait_ge(S[f"xx_in{slot}"], 16 * (r + 1))
                    need(dve, S["o_tp"], n - 3)
                    for j in range(T // 2):
                        ins = V.tensor_scalar(h[:, slot, j, :], xb[:, eighth(u, 2), j, :],
                                              rstd1[:, bass.ds(n * T + j, 1)], nb1[:, bass.ds(n * T + j, 1)],
                                              ALU.mult, ALU.add)
                    ins.then_inc(S["o_h2"], 1)
                n = grp(i, u, 4)
                if n:
                    n, slot, r = n
                    dve.wait_ge(S["o_tp"], n + 1)
                    need(dve, S["o_mm"], n - 1)
                    V.tensor_scalar(hT[:, slot % 2, :], bank[6 + slot % 2][:, :], 0.0, None,
                                    ALU.max).then_inc(S["o_hT"], 1)
                n = grp(i, u, 7)
                if n:
                    n, slot, r = n
                    dve.wait_ge(S["o_nrm"], n + 1)
                    V.reciprocal(inv[:, slot, :], nrm[:, slot, :]).then_inc(S["o_inv"], 1)
                n = grp(i, u, 7)
                if n:
                    n, slot, r = n
                    dve.wait_ge(S["o_inv"], n + 1)
                    for j in range(T):
                        ins = V.scalar_tensor_tensor(x1[:, slot, j, :], x1[:, slot, j, :],
                                                     inv[:, slot, j:j + 1], xb[:, eighth(u, 7), j, :],
                                                     ALU.mult, ALU.add)
                    ins.then_inc(S["o_y"], 1)

            for k in range(4):
                dve.wait_ge(S[f"x1_out{k}"], 16 * LAPS[k])
                dve.wait_ge(S[f"t1_out{k}"], 16 * LAPS[k])
            with dve.If(bad_n > 0):
                general_vector(dve, 1)
            rounds(dve, layer1_step, 7)

        @block.tensor
        def _(pe):
            mm = nc.tensor.matmul
            pe.wait_ge(S["started_rdy"], 1)
            pe.wait_ge(S["ones_rdy"], 1)
            K = TILES // 4
            for c in range(4):
                ins = mm(bank[0][:, 0:TILES + 1], ones_b[0:K, :], started[:, c, :], start=c == 0, stop=c == 3)
            ins.then_inc(S["a_psum"], 1)

            def histogram(n, k):
                g, slot, r = n
                pe.wait_ge(S["hot_rdy"], g + (k * GROUPS + 1))
                for j in range(T):
                    for half in range(LOW // P):
                        ins = mm(bank[2 + k][:, half * HIGH:(half + 1) * HIGH],
                                 low_hot[:, slot % 2, half * P:(half + 1) * P, j], high_hot[:, slot % 2, :, j],
                                 start=isinstance(g, int) and g == 0 and j == 0 and half == 0,
                                 stop=isinstance(g, int) and g == GROUPS - 1 and j == T - 1,
                                 skip_group_check=True)
                ins.then_inc(S["hist_done"], 1)

            def send_step(i, u):
                g = grp(i, u, 0)
                if g:
                    histogram(g, 0)

            rounds(pe, send_step, 0)

            def node_step(i, u):
                g = grp(i, u, 3)
                if g:
                    g, slot, r = g
                    pe.wait_ge(S["n_h"], g + 1)
                    need(pe, S["n_hT"], g - 1)
                    for j in range(T):
                        ins = nc.tensor.transpose(bank[4 + slot % 2][:, j * P:(j + 1) * P], h[:, slot, j, :],
                                                  ident[:, :])
                    ins.then_inc(S["n_tp"], 1)
                g = grp(i, u, 5)
                if g:
                    g, slot, r = g
                    pe.wait_ge(S["n_hT"], g + 1)
                    need(pe, S["n_evac"], g - 1)
                    affine(bank[6 + slot % 2], 0, [(hT[:, slot % 2, :], wn[:, :])], S["n_mm"])
                g = grp(i, u, 0)
                if g:
                    histogram(g, 1)

            def affine(out_bank, b, pairs, done):
                if b is not None:
                    mm(out_bank[:, :], ones3[:, :], bias4[:, b, :, :].rearrange("k j f -> k (j f)"),
                       start=True, stop=False, skip_group_check=True)
                for j in range(T):
                    for rows, w in pairs:
                        ins = mm(out_bank[:, j * D:(j + 1) * D], rows[:, j * P:(j + 1) * P], w,
                                 start=b is None and j == 0 and w is pairs[0][1], stop=True,
                                 skip_group_check=True)
                ins.then_inc(done, 1)

            pe.wait_ge(S["consts_in"], 16 * 15)
            pe.wait_ge(S["bias_rdy"], 1)
            rounds(pe, node_step, 5)
            pe.wait_ge(S["bad_psum"], 1)
            mm(bank[1][:, 0:1], ones[:, :], bad[:, 4:5], start=True, stop=True).then_inc(S["bad_psum"], 1)
            pe.wait_ge(S["chosen_rdy"], 1)
            pe.wait_ge(S["n_hT"], GROUPS)
            pe.wait_ge(S["n_evac"], GROUPS)
            for k in range(SPAN):
                for part in range(2):
                    for c in range(4):
                        ins = mm(bank[5 + k][:, 0:TILES], dst_rows[:, part, c, :], chosen[:, k, c, :],
                                 start=part == 0 and c == 0, stop=part == 1 and c == 3)
            ins.then_inc(S["rel_psum"], 1)

            def places(n):
                return nc.values_load_multi_w_load_instructions(
                    ring_at[0:1, bass.ds(n * T, T)], engines=(pe.engine,), min_val=0,
                    max_val=(RING - 1) * D)[1]

            def third_of(n):
                return pe.value_load(wide[0:1, bass.ds(n, 1)], min_val=0, max_val=1)

            def sums(place, third, par, out_bank, done):
                def add(j, k):
                    return mm(out_bank[:, j * D:(j + 1) * D], pick[:, par, k * T + j, :],
                              ring_flat[:, k * D:][:, bass.ds(place[j], D)],
                              start=j == 0 and k == 0, stop=True, skip_group_check=True)

                for j in range(T):
                    add(j, 0)
                    if j < T - 1:
                        add(j, 1)
                with pe.If(third > 0):
                    for j in range(T):
                        add(j, 2)
                add(T - 1, 1).then_inc(done, 1)

            def layer0_step(i, u):
                g = grp(i, u, 0)
                if g:
                    g, slot, r = g
                    pe.wait_ge(S[f"e_in{slot}"], 16 * (r + 1))
                    need(pe, S["msg_rdy"], g - 3)
                    affine(edge_bank(slot), 1, [(edge[:, slot, :], we[:, :])], S["emm_done"])
                n = grp(i, u, LAG)
                if n:
                    place = places(n[0])
                g = grp(i, u, 1)
                if g:
                    g, slot, r = g
                    pe.wait_ge(S[f"g_in{slot}"], 64 * (r + 1))
                    mm(edge_bank(slot)[:, :], ident[:, :], gath[:, eighth(u, 1), :, 0:D], start=False, stop=True,
                       skip_group_check=True).then_inc(S["sum_rdy"], 1)
                if n:
                    third = third_of(n[0])
                    n, slot, r = n
                    pe.wait_ge(S["pick_rdy"], n + 1)
                    if isinstance(n, int):
                        pe.wait_ge(S["msg_rdy"], min(n + REACH, GROUPS))
                    else:
                        pe.wait_ge(S["msg_rdy"], n + REACH)
                    need(pe, S["v_rdy"], n - 1)
                    sums(place, third, slot % 2, bank[2 + slot % 2], S["seg_done"])

            pe.wait_ge(S["tables_rdy"], 2)
            pe.wait_ge(S["rel_used"], 1)
            bad_n = flag_of(pe)
            with pe.If(bad_n > 0):
                pe.wait_ge(S["n_evac"], GROUPS)
                general_products(pe, 0)
            rounds(pe, layer0_step, LAG)

            def layer1_step(i, u):
                m = grp(i, u, 1)
                if m:
                    third = third_of(m[0])
                n = grp(i, u, 5)
                if n:
                    n, slot, r = n
                    pe.wait_ge(S["o_hT"], n + 1)
                    pe.wait_ge(S["o_aT"], n + 1)
                    need(pe, S["o_sum"], n - 1)
                    affine(bank[2 + slot % 2], None, [(hT[:, slot % 2, :], w1[:, 0, :]),
                                                   (aT[:, slot % 2, :], w1[:, 1, :])], S["o_mm"])
                if m:
                    place = places(m[0])
                n = grp(i, u, 3)
                if n:
                    n, slot, r = n
                    pe.wait_ge(S["o_h"], n + 1)
                    pe.wait_ge(S["o_h2"], n + 1)
                    pe.wait_ge(S["o_agg"], n + 1)
                    need(pe, S["o_hT"], n - 1)
                    need(pe, S["o_aT"], n - 1)
                    for j in range(T):
                        nc.tensor.transpose(bank[6 + slot % 2][:, j * P:(j + 1) * P], h[:, slot, j, :],
                                            ident[:, :])
                        ins = nc.tensor.transpose(bank[slot % 2][:, j * P:(j + 1) * P],
                                                  agg[:, slot % 2, j, :], ident[:, :])
                    ins.then_inc(S["o_tp"], 1)
                if m:
                    n, slot, r = m
                    pe.wait_ge(S["o_pick"], n + 1)
                    if isinstance(n, int) and n == 0:
                        for k in range(REACH - 1):
                            pe.wait_ge(S[f"r_in{k}"], 64)
                    if not (isinstance(n, int) and n + REACH > GROUPS):
                        last = slot + REACH - 1
                        pe.wait_ge(S[f"r_in{last % 4}"], 64 * (r + last // 4 + 1))
                    if isinstance(n, int):
                        pe.wait_ge(S["o_again"], min(n + REACH - 1, GROUPS - 1) // 8 + 1)
                    elif eighth(u, 2 - REACH) == 0:
                        pe.wait_ge(S["o_again"], i + (u + REACH - 2) // 8 + 1)
                    need(pe, S["o_agg"], n - 1)
                    sums(place, third, slot % 2, bank[4 + slot % 2], S["o_seg"])

            pe.wait_ge(S["v_rdy"], GROUPS)
            pe.wait_ge(S["n_evac"], GROUPS)
            with pe.If(bad_n > 0):
                general_products(pe, 1)
            rounds(pe, layer1_step, 6)

        @block.scalar
        def _(act):
            A = nc.scalar.activation
            act.wait_ge(S["deg_sum"], 1)
            A(dsq[:, 0, :], deg[:, 0, :], ACT.Sqrt).then_inc(S["deg_sqrt"], 1)

            def node_step(i, u):
                g = grp(i, u, 1)
                if g:
                    g, slot, r = g
                    act.wait_ge(S["n_stats"], g + 1)
                    A(sd[:, slot, :], mv[:, slot, :, 1], ACT.Sqrt, bias=eps_t[:, :]).then_inc(S["n_sd"], 1)
                g = grp(i, u, 6)
                if g:
                    g, slot, r = g
                    act.wait_ge(S["n_mm"], g + 1)
                    need(act, S[f"t0_out{slot}"], 16 * r)
                    A(ya[:, slot, :, 0:D], bank[6 + slot % 2][:, :].rearrange("p (j f) -> p j f", f=D),
                      ACT.Copy).then_inc(S["n_evac"], 1)
                g = grp(i, u, 4)
                if g:
                    g, slot, r = g
                    act.wait_ge(S["n_tp"], g + 1)
                    need(act, S["n_mm"], g - 1)
                    A(hT[:, slot % 2, :], bank[4 + slot % 2][:, :], ACT.Copy).then_inc(S["n_hT"], 1)
                g = grp(i, u, 2)
                if g:
                    g, slot, r = g
                    act.wait_ge(S["n_coef"], g + 1)
                    need(act, S["n_tp"], g - 3)
                    for j in range(T):
                        ins = A(h[:, slot, j, :], xb[:, eighth(u, 2), j, :], ACT.Relu,
                                bias=nb[:, slot, j:j + 1], scale=rs[:, slot, j:j + 1])
                    ins.then_inc(S["n_h"], 1)
                g = grp(i, u, 6)
                if g:
                    g, slot, r = g
                    act.wait_ge(S["n_evac"], g + 1)
                    act.wait_ge(S["n_col"], g + 1)
                    act.dma_start(rows4(table0, g), ya[:, slot, :, :]).then_inc(S[f"t0_out{slot}"], 16)

            rounds(act, node_step, 6)
            act.wait_ge(S["deg_sum"], 2)
            A(dsq[:, 1:3, :], deg[:, 1:3, :], ACT.Sqrt).then_inc(S["deg_sqrt"], 1)

            def layer0_step(i, u):
                n = grp(i, u, LAG)
                if n:
                    n, slot, r = n
                    act.wait_ge(S[f"y_in{slot}"], 16 * (r + 1))
                    need(act, S["v_rdy"], n - 1)
                    for j in range(T):
                        ins = A(q[:, slot % 2, j, :], ya[:, slot, j, 0:D], ACT.Relu,
                                scale=rinv[:, bass.ds(n * T + j, 1)])
                    ins.then_inc(S["q_rdy"], 1)
                g = grp(i, u, 1)
                if g:
                    g, slot, r = g
                    act.wait_ge(S["sum_rdy"], g + 1)
                    need(act, S["seg_done"], g - 5)
                    for j in range(T):
                        for place in ring_places_of(u, 1, j):
                            ins = A(ring[:, place, :], edge_bank(slot)[:, j * D:(j + 1) * D], ACT.Relu,
                                    scale=gath[:, eighth(u, 1), j, D:D + 1])
                    ins.then_inc(S["msg_rdy"], 1)
                n = grp(i, u, LAG + 2)
                if n:
                    n, slot, r = n
                    act.wait_ge(S["l_stats"], n + 1)
                    A(sd[:, slot, :], mv[:, slot, :, 1], ACT.Sqrt, bias=eps_t[:, :]).then_inc(S["l_sd"], 1)
                    act.wait_ge(S["x1_rdy"], n + 1)
                    act.dma_start(rows4(x1_dram, n), x1[:, slot, :, :]).then_inc(S[f"x1_out{slot}"], 16)
                n = grp(i, u, LAG + 3)
                if n:
                    n, slot, r = n
                    act.wait_ge(S["l_coef"], n + 1)
                    need(act, S[f"t1_out{slot}"], 16 * r)
                    for j in range(T):
                        ins = A(h[:, slot, j, :], x1[:, slot, j, :], ACT.Relu, bias=bi1[:, slot, j:j + 1],
                                scale=sc1[:, slot, j:j + 1])
                    ins.then_inc(S["t1_rdy"], 1)
                    act.wait_ge(S["t1_rdy"], n + 1)
                    act.dma_start(rows4(table1, n), h[:, slot, :, :]).then_inc(S[f"t1_out{slot}"], 16)

            act.wait_ge(S["tables_rdy"], 2)
            act.wait_ge(S["n_tp"], GROUPS)
            bad_n = flag_of(act)
            with act.If(bad_n > 0):
                general_messages(act)
            rounds(act, layer0_step, LAG + 3)

            def repeat_first(r_in, value):
                act.wait_ge(r_in, value)
                A(ring[:, RING:, :], ring[:, 0:SPAN - 1, :], ACT.Copy).then_inc(S["o_again"], 1)

            def layer1_step(i, u):
                g = grp(i, u, -3)
                if g and eighth(u, -3) == 0:
                    g, slot, r = g
                    repeat_first(S[f"r_in{slot}"], 64 * (r + 1))
                n = grp(i, u, 2)
                if n:
                    n, slot, r = n
                    act.wait_ge(S["o_seg"], n + 1)
                    need(act, S["o_tp"], n - 1)
                    for j in range(T):
                        ins = A(agg[:, slot % 2, j, :], bank[4 + slot % 2][:, j * D:(j + 1) * D], ACT.Copy,
                                scale=norm1[:, bass.ds(n * T + j, 1)])
                    ins.then_inc(S["o_agg"], 1)
                n = grp(i, u, 8)
                if n:
                    n, slot, r = n
                    act.wait_ge(S["o_y"], n + 1)
                    act.dma_start(rows4(out, n), x1[:, slot, :, :]).then_inc(S[f"y_out{slot}"], 16)
                n = grp(i, u, 2)
                if n:
                    n, slot, r = n
                    act.wait_ge(S[f"xx_in{slot}"], 16 * (r + 1))
                    for j in range(T // 2, T):
                        ins = A(h[:, slot, j, :], xb[:, eighth(u, 2), j, :], ACT.Identity,
                                bias=nb1[:, bass.ds(n * T + j, 1)], scale=rstd1[:, bass.ds(n * T + j, 1)])
                    ins.then_inc(S["o_h"], 1)
                n = grp(i, u, 6)
                if n:
                    n, slot, r = n
                    act.wait_ge(S["o_sum"], n + 1)
                    need(act, S["o_inv"], n - 3)
                    for j in range(T):
                        ins = A(junk[:, j, :], x1[:, slot, j, :], ACT.Square,
                                accum_out=ss[:, slot, j:j + 1])
                    ins.then_inc(S["o_sq"], 1)
                n = grp(i, u, 4)
                if n:
                    n, slot, r = n
                    act.wait_ge(S["o_tp"], n + 1)
                    need(act, S["o_mm"], n - 1)
                    A(aT[:, slot % 2, :], bank[slot % 2][:, :], ACT.Copy).then_inc(S["o_aT"], 1)
                n = grp(i, u, 6)
                if n:
                    n, slot, r = n
                    act.wait_ge(S["o_sq"], n + 1)
                    A(nrm[:, slot, :], ss[:, slot, :], ACT.Sqrt).then_inc(S["o_nrm"], 1)

            for k in range(4):
                act.wait_ge(S[f"x1_out{k}"], 16 * LAPS[k])
                act.wait_ge(S[f"t1_out{k}"], 16 * LAPS[k])
            repeat_first(S["r_in0"], 64)
            rounds(act, layer1_step, 8)
            for k in range(4):
                act.wait_ge(S[f"y_out{k}"], 16 * LAPS[k])


def kernel(x, src, dst, edge_attr_128, L0_gnn_W_node, L0_gnn_b_node, L0_gnn_W_edge, L0_gnn_b_edge,
           L0_gnn_root_emb, L1_gnn_weight, L1_gnn_bias):
    import numpy as np
    import concourse.bacc as bacc
    from concourse.bass_utils import run_bass_kernel_spmd

    pad = np.arange(NODES, ROWS, dtype=np.int32)
    zero_rows = np.zeros((ROWS - NODES, D), np.float32)
    src_all = np.concatenate([np.asarray(src), pad])
    dst_all = np.concatenate([np.asarray(dst), pad])
    dst_tiles = dst_all.reshape(TILES, P)
    edges = np.concatenate([np.asarray(edge_attr_128), zero_rows])
    tiles = np.arange(TILES + 4, dtype=np.float32)

    def across(row):
        return np.ascontiguousarray(np.broadcast_to(row, (P, row.shape[-1])))

    arrays = {
        "x": np.concatenate([np.asarray(x), zero_rows]),
        "edgeT": np.ascontiguousarray(edges.T),
        "srcT": np.ascontiguousarray(src_all.reshape(TILES, P).T),
        "dstT": np.ascontiguousarray(dst_tiles.T),
        "dst_cur": dst_all.reshape(P, TILES),
        "dst_next": np.concatenate([dst_all[1:], dst_all[-1:]]).reshape(P, TILES),
        "dst_first": np.ascontiguousarray(dst_tiles[:, 0]).reshape(TILES // 4, 4),
        "group_tile": across(np.float32(T) * np.arange(GROUPS, dtype=np.float32).repeat(T)),
        "tile_no": np.arange(TILES, dtype=np.float32).reshape(TILES // 4, 1, 4)
        - np.arange(SPAN, dtype=np.float32).reshape(1, SPAN, 1),
        "dst_rows": dst_all.reshape(TILES // 4, 4, P),
        "w_node": np.asarray(L0_gnn_W_node), "b_node": np.asarray(L0_gnn_b_node).reshape(1, D),
        "w_edge": np.asarray(L0_gnn_W_edge), "b_edge": np.asarray(L0_gnn_b_edge).reshape(1, D),
        "root": np.asarray(L0_gnn_root_emb), "w_out": np.asarray(L1_gnn_weight),
        "b_out": across(np.asarray(L1_gnn_bias)),
        "ident": np.eye(P, dtype=np.float32),
        "iota": across(tiles),
        "tile_base": across(np.float32(P) * tiles),
        "before": np.concatenate([np.tri(P, k=-1, dtype=np.float32),
                                  np.arange(P, dtype=np.float32).reshape(P, 1)], 1),
    }
    nc = bacc.Bacc("TRN2", target_bir_lowering=False, num_devices=1)
    aps = [nc.dram_tensor(f"in_{k}", a.shape, mybir.dt.from_np(a.dtype), kind="ExternalInput").ap()
           for k, a in arrays.items()]
    out = nc.dram_tensor("out", (ROWS, D), mybir.dt.float32, kind="ExternalOutput").ap()
    gnn_kernel(nc, *aps, out)
    r = run_bass_kernel_spmd(nc, [{f"in_{k}": a for k, a in arrays.items()}], core_ids=[0])
    return r.results[0]["out"][:NODES]
```
